# Optimizing a Trainium2 kernel written in Bass

```python
import numpy as np
import jax
import jax.numpy as jnp

def _softmax(x, axis=-1):
    return jax.nn.softmax(x, axis=axis)

def _gelu(x):
    return jax.nn.gelu(x, approximate=True)

def _silu(x):
    return jax.nn.silu(x)

def _sigmoid(x):
    return jax.nn.sigmoid(x)

def _layernorm(x, axis=-1, eps=1e-05):
    m = jnp.mean(x, axis=axis, keepdims=True)
    v = jnp.var(x, axis=axis, keepdims=True)
    return (x - m) / jnp.sqrt(v + eps)

def _scatter_add(tgt, idx, src, axis=0):
    return tgt.at[idx].add(src)

def _segment_sum(src, seg, n):
    return jax.ops.segment_sum(src, seg, n)
kernel_name = 'mk_seq_preln_d1_jaxref_r8_a76617'

def setup_inputs(seed: int=0):
    np.random.seed(seed)
    _w = jnp.asarray

    def _L0_attn_setup():
        import jax, jax.numpy as jnp
        import numpy as np
        HIDDEN = 128
        HEADS = 16
        HEAD_DIM = HIDDEN // HEADS
        B, S = (4, 256)
        key = jax.random.key(seed)
        ks = jax.random.split(key, 10)
        scale = 1.0 / np.sqrt(HIDDEN)

        def lin(k):
            return jax.random.uniform(k, (HIDDEN, HIDDEN), jnp.float32, -scale, scale)
        return {'x': jax.random.normal(ks[0], (B, S, HIDDEN), jnp.float32), 'Wq': lin(ks[1]), 'bq': jnp.zeros((HIDDEN,), jnp.float32), 'Wk': lin(ks[2]), 'bk': jnp.zeros((HIDDEN,), jnp.float32), 'Wv': lin(ks[3]), 'bv': jnp.zeros((HIDDEN,), jnp.float32), 'Wo': lin(ks[4]), 'bo': jnp.zeros((HIDDEN,), jnp.float32), 'head_mask': jnp.ones((HEADS,), jnp.float32)}
    _L0_attn_in = _L0_attn_setup()

    def _L0_ffn_setup():
        import jax, jax.numpy as jnp
        import numpy as np
        import math
        N_EMBD = 128
        HIDDEN = 4 * N_EMBD
        N_EXPERTS = 8
        TOP_K = 2
        B, T = (4, 256)

        def new_gelu(x):
            c = math.sqrt(2.0 / math.pi)
            return 0.5 * x * (1.0 + jnp.tanh(c * (x + 0.044715 * x * x * x)))

        def _moe_forward(x, Wfc_s, bfc_s, Wproj_s, bproj_s, Wr, Wfc, bfc, Wproj, bproj):
            Bb, Tt, C = x.shape
            xf = x.reshape(Bb * Tt, C)
            N = Bb * Tt
            shared = new_gelu(xf @ Wfc_s + bfc_s) @ Wproj_s + bproj_s
            logits = xf @ Wr
            probs = jax.nn.softmax(logits, axis=-1)
            topk_p, topk_i = jax.lax.top_k(probs, TOP_K)
            topk_p = topk_p / jnp.sum(topk_p, axis=-1, keepdims=True)
            gate = jnp.zeros((N, N_EXPERTS), dtype=xf.dtype)
            gate = gate.at[jnp.arange(N)[:, None], topk_i].add(topk_p)
            routed = jnp.zeros_like(xf)
            for e in range(N_EXPERTS):
                h = new_gelu(xf @ Wfc[e] + bfc[e]) @ Wproj[e] + bproj[e]
                routed = routed + h * gate[:, e:e + 1]
            return (shared + routed).reshape(Bb, Tt, C)
        key = jax.random.key(seed)
        ks = jax.random.split(key, 10)
        s = 0.02
        return {'x': jax.random.normal(ks[0], (B, T, N_EMBD), dtype=jnp.float32), 'Wfc_s': jax.random.normal(ks[1], (N_EMBD, HIDDEN), dtype=jnp.float32) * s, 'bfc_s': jnp.zeros((HIDDEN,), dtype=jnp.float32), 'Wproj_s': jax.random.normal(ks[2], (HIDDEN, N_EMBD), dtype=jnp.float32) * s, 'bproj_s': jnp.zeros((N_EMBD,), dtype=jnp.float32), 'Wr': jax.random.normal(ks[3], (N_EMBD, N_EXPERTS), dtype=jnp.float32) * s, 'Wfc': jax.random.normal(ks[4], (N_EXPERTS, N_EMBD, HIDDEN), dtype=jnp.float32) * s, 'bfc': jnp.zeros((N_EXPERTS, HIDDEN), dtype=jnp.float32), 'Wproj': jax.random.normal(ks[5], (N_EXPERTS, HIDDEN, N_EMBD), dtype=jnp.float32) * s, 'bproj': jnp.zeros((N_EXPERTS, N_EMBD), dtype=jnp.float32)}
    _L0_ffn_in = _L0_ffn_setup()
    _d = {'L0_attn_x': _L0_attn_in['x'], 'L0_attn_Wq': _L0_attn_in['Wq'], 'L0_attn_bq': _L0_attn_in['bq'], 'L0_attn_Wk': _L0_attn_in['Wk'], 'L0_attn_bk': _L0_attn_in['bk'], 'L0_attn_Wv': _L0_attn_in['Wv'], 'L0_attn_bv': _L0_attn_in['bv'], 'L0_attn_Wo': _L0_attn_in['Wo'], 'L0_attn_bo': _L0_attn_in['bo'], 'L0_attn_head_mask': _L0_attn_in['head_mask'], 'L0_ffn_Wfc_s': _L0_ffn_in['Wfc_s'], 'L0_ffn_bfc_s': _L0_ffn_in['bfc_s'], 'L0_ffn_Wproj_s': _L0_ffn_in['Wproj_s'], 'L0_ffn_bproj_s': _L0_ffn_in['bproj_s'], 'L0_ffn_Wr': _L0_ffn_in['Wr'], 'L0_ffn_Wfc': _L0_ffn_in['Wfc'], 'L0_ffn_bfc': _L0_ffn_in['bfc'], 'L0_ffn_Wproj': _L0_ffn_in['Wproj'], 'L0_ffn_bproj': _L0_ffn_in['bproj']}
    _x0 = _d['L0_attn_x']
    _d['L0_attn_x'] = jax.random.normal(jax.random.fold_in(jax.random.key(seed), 1), (8, 512, 128), dtype=_x0.dtype)
    del _x0
    return _d

def reference(L0_attn_x, L0_attn_Wq, L0_attn_bq, L0_attn_Wk, L0_attn_bk, L0_attn_Wv, L0_attn_bv, L0_attn_Wo, L0_attn_bo, L0_attn_head_mask, L0_ffn_Wfc_s, L0_ffn_bfc_s, L0_ffn_Wproj_s, L0_ffn_bproj_s, L0_ffn_Wr, L0_ffn_Wfc, L0_ffn_bfc, L0_ffn_Wproj, L0_ffn_bproj):

    def _L0_attn_ref(x, Wq, bq, Wk, bk, Wv, bv, Wo, bo, head_mask):
        import jax, jax.numpy as jnp
        import numpy as np
        HIDDEN = 128
        HEADS = 16
        HEAD_DIM = HIDDEN // HEADS
        B, S = (4, 256)
        b, s, _ = x.shape
        q = (x @ Wq.T + bq).reshape(b, s, HEADS, HEAD_DIM)
        k = (x @ Wk.T + bk).reshape(b, s, HEADS, HEAD_DIM)
        v = (x @ Wv.T + bv).reshape(b, s, HEADS, HEAD_DIM)
        attn = jnp.einsum('bqhd,bkhd->bhqk', q, k) / np.sqrt(HEAD_DIM).astype(np.float32)
        attn = jax.nn.softmax(attn, axis=-1)
        attn = attn * head_mask[None, :, None, None]
        out = jnp.einsum('bhqk,bkhd->bqhd', attn, v).reshape(b, s, HIDDEN)
        return out @ Wo.T + bo

    def _L0_ffn_ref(x, Wfc_s, bfc_s, Wproj_s, bproj_s, Wr, Wfc, bfc, Wproj, bproj):
        import jax, jax.numpy as jnp
        import numpy as np
        import math
        N_EMBD = 128
        HIDDEN = 4 * N_EMBD
        N_EXPERTS = 8
        TOP_K = 2
        B, T = (4, 256)

        def new_gelu(x):
            c = math.sqrt(2.0 / math.pi)
            return 0.5 * x * (1.0 + jnp.tanh(c * (x + 0.044715 * x * x * x)))

        def _moe_forward(x, Wfc_s, bfc_s, Wproj_s, bproj_s, Wr, Wfc, bfc, Wproj, bproj):
            Bb, Tt, C = x.shape
            xf = x.reshape(Bb * Tt, C)
            N = Bb * Tt
            shared = new_gelu(xf @ Wfc_s + bfc_s) @ Wproj_s + bproj_s
            logits = xf @ Wr
            probs = jax.nn.softmax(logits, axis=-1)
            topk_p, topk_i = jax.lax.top_k(probs, TOP_K)
            topk_p = topk_p / jnp.sum(topk_p, axis=-1, keepdims=True)
            gate = jnp.zeros((N, N_EXPERTS), dtype=xf.dtype)
            gate = gate.at[jnp.arange(N)[:, None], topk_i].add(topk_p)
            routed = jnp.zeros_like(xf)
            for e in range(N_EXPERTS):
                h = new_gelu(xf @ Wfc[e] + bfc[e]) @ Wproj[e] + bproj[e]
                routed = routed + h * gate[:, e:e + 1]
            return (shared + routed).reshape(Bb, Tt, C)
        return _moe_forward(x, Wfc_s, bfc_s, Wproj_s, bproj_s, Wr, Wfc, bfc, Wproj, bproj)
    x = L0_attn_x
    x = x + _L0_attn_ref(_layernorm(x, axis=-1), L0_attn_Wq, L0_attn_bq, L0_attn_Wk, L0_attn_bk, L0_attn_Wv, L0_attn_bv, L0_attn_Wo, L0_attn_bo, L0_attn_head_mask)
    x = x + _L0_ffn_ref(_layernorm(x, axis=-1), L0_ffn_Wfc_s, L0_ffn_bfc_s, L0_ffn_Wproj_s, L0_ffn_bproj_s, L0_ffn_Wr, L0_ffn_Wfc, L0_ffn_bfc, L0_ffn_Wproj, L0_ffn_bproj)
    return x

_drawn_inputs = setup_inputs


def setup_inputs(seed=0):
    import zlib

    import numpy as np

    out = dict(_drawn_inputs(seed))
    spreads = {'L0_attn_bq': (0.0, 0.8),
     'L0_attn_bk': (0.0, 0.8),
     'L0_attn_bv': (0.0, 0.1),
     'L0_attn_bo': (0.0, 0.1),
     'L0_ffn_bfc_s': (0.0, 0.308),
     'L0_ffn_bproj_s': (0.0, 0.1),
     'L0_ffn_bfc': (0.0, 0.486),
     'L0_ffn_bproj': (0.0, 0.1)}
    factors = {'L0_attn_Wq': 4.282, 'L0_attn_Wk': 4.182, 'L0_attn_Wv': 2.815}
    for name, (base, spread) in spreads.items():
        noise = np.random.default_rng([zlib.crc32(name.encode()), seed]).standard_normal(out[name].shape)
        drawn = base * np.exp(spread * noise) if base else spread * noise
        out[name] = jnp.asarray(drawn.astype(out[name].dtype))
    for name, factor in factors.items():
        out[name] = (out[name] * factor).astype(out[name].dtype)
    return out
```

```python
import concourse.bass as bass
from concourse import mybir
from contextlib import ExitStack

B, S, C = 8, 512, 128
H, D = 16, 8
J = 4
HG = H // J
P = 128
NT = S // P
PARTS = 3
PR = PARTS * D
KR = PARTS * PR
SR = KR + PARTS
E, F = 8, 512
NE = E + 1
FC = F // P
EPS = 1e-5
NG = B * HG


def block_kernel(nc, x, WqT, WkT, WvT, WoT, bq, bk, bv, bo, head_mask, W1, b1, W2, b2, Wr, ident, iota8, out):
    f32, bf16, u32 = mybir.dt.float32, mybir.dt.bfloat16, mybir.dt.uint32
    ALU, ACT, AX = mybir.AluOpType, mybir.ActivationFunctionType, mybir.AxisListType

    q_scr = nc.dram_tensor("q_scr", (B, H * D, PARTS * S), bf16, kind="Internal").ap()
    k_scr = [nc.dram_tensor(f"k_scr{r}", (B, H * D, PARTS * S), bf16, kind="Internal").ap() for r in range(PARTS)]

    ctx = ExitStack()
    with ctx:
        def sb(name, shape, dt=f32):
            return ctx.enter_context(nc.sbuf_tensor(name, shape, dt))

        def sem(name):
            return ctx.enter_context(nc.semaphore(name))

        wq_sb, wk_sb, wv_sb = sb("wq_sb", [P, C]), sb("wk_sb", [P, C]), sb("wv_sb", [P, C])
        wo_sb = sb("wo_sb", [P, HG, C])
        bq_sb, bk_sb = sb("bq_sb", [P, 1]), sb("bk_sb", [P, 1])
        bv_sb, bo_sb = sb("bv_sb", [P, C]), sb("bo_sb", [P, C])
        mask_sb = sb("mask_sb", [P, HG])
        w1_sb, b1_sb = sb("w1_sb", [P, NE, F]), sb("b1_sb", [P, NE, FC])
        w2_sb = sb("w2_sb", [P, NE, FC, C])
        b2_sb = sb("b2_sb", [P, C])
        wr_sb = sb("wr_sb", [P, E])
        id_sb, id_bf = sb("id_sb", [P, P]), sb("id_bf", [P, P], bf16)
        iota_sb = sb("iota_sb", [P, E])
        neg_half, e_const = sb("neg_half", [P, B * NT]), sb("e_const", [P, NT])
        x_sb = sb("x_sb", [P, B * NT, C])
        stats = sb("stats", [P, B * NT, 6])
        mean, mean_d = sb("mean", [P, B * NT]), sb("mean_d", [P, B * NT])
        dev, mean_d2 = sb("dev", [P, B * NT]), sb("mean_d2", [P, B * NT])
        var_eps, rstd = sb("var_eps", [P, B * NT]), sb("rstd", [P, B * NT])
        xn = sb("xn", [P, 2, NT, C])
        xnT = sb("xnT", [P, 2, S])
        qk32 = sb("qk32", [P, 2, 2, S])
        rest = sb("rest", [P, 2, S])
        parts = sb("parts", [P, 2, 2, PARTS, S], bf16)
        v_all = sb("v_all", [P, B, NT, C])
        q_op = [sb(f"q_op{g}", [SR, J, S], bf16) for g in range(HG)]
        k_op = [sb(f"k_op{g}", [SR, J, S], bf16) for g in range(HG)]
        v_op = sb("v_op", [P, HG, NT, J, 32])
        mx = sb("mx", [P, 2, J * NT])
        mx_rest = sb("mx_rest", [P, J * NT])
        mx_parts = sb("mx_parts", [P, P], bf16)
        mxT = sb("mxT", [PARTS * J * NT, 2, P], bf16)
        probs = sb("probs", [P, 2, J, 2 * S])
        o_t = sb("o_t", [P, S // 32, 32])
        o_rec = sb("o_rec", [P, S // 32])
        o_sb = sb("o_sb", [P, HG, S])
        y = sb("y", [P, 2, NT, C])
        y_rstd = sb("y_rstd", [P, NT])
        yT = sb("yT", [P, 2, S])
        logits, top1, top8 = sb("logits", [P, NT, E]), sb("top1", [P, NT]), sb("top8", [P, NT, 8])
        top_i, top_if = sb("top_i", [P, NT, 8], u32), sb("top_if", [P, NT, 2])
        l_diff, l_exp, l_sum = sb("l_diff", [P, NT]), sb("l_exp", [P, NT]), sb("l_sum", [P, NT])
        top_p = sb("top_p", [P, 2, NT])
        pick = sb("pick", [P, 2, NT, E])
        gate = sb("gate", [P, 2, NT, P])
        gateT = sb("gateT", [P, 2, S])
        hid = probs[:, :, :, 0:S]
        ps = ctx.enter_context(nc.psum_tensor("ps", [P, 8, 512], f32))

        s_x, s_w, s_wffn = sem("x_loaded"), sem("weights_loaded"), sem("ffn_weights_loaded")
        s_const, s_idbf, s_pad = sem("constants_set"), sem("id_bf_set"), sem("padding_set")
        s_st, s_ve, s_rstd = sem("ln1_steps"), sem("ln1_var_eps"), sem("ln1_rstd")
        s_xn, s_xnTp, s_xnT = sem("xn_ready"), sem("xnT_in_psum"), sem("xnT_ready")
        s_qp, s_kp, s_vp = sem("q_in_psum"), sem("k_in_psum"), sem("v_in_psum")
        s_qk32, s_hi, s_rest = sem("qk32_ready"), sem("first_parts_ready"), sem("rest_ready")
        s_mid, s_lo, s_v, s_scr = sem("second_parts_ready"), sem("third_parts_ready"), sem("v_stored"), [sem("scratch_stored0"), sem("scratch_stored1")]
        s_ld = [sem(f"qk_op_loaded{g}") for g in range(HG)]
        s_sh = [sem(f"shift_rows_loaded{g}") for g in range(HG)]
        s_sa, s_max = sem("row_scores_in_psum"), sem("row_maxima_taken")
        s_ms, s_msp, s_mxTp, s_mxT = sem("max_split_steps"), sem("max_parts_ready"), sem("mxT_in_psum"), sem("mxT_ready")
        s_sb, s_exp = sem("key_scores_in_psum"), sem("probs_ready")
        s_vop, s_pv = sem("v_op_ready"), sem("pv_halves_done")
        s_ot, s_orec, s_onrm, s_o = sem("o_transposed"), sem("o_reciprocal"), sem("o_normalised"), sem("o_ready")
        s_xbo, s_ap, s_x2 = sem("x_plus_bias"), sem("attention_projected"), sem("x2_ready")
        s_yst, s_yve, s_yrs = sem("ln2_steps"), sem("ln2_var_eps"), sem("ln2_rstd")
        s_y, s_yTp, s_yT = sem("y_ready"), sem("yT_in_psum"), sem("yT_ready")
        s_lgp, s_rt, s_gd, s_ge = sem("logits_in_psum"), sem("router_steps"), sem("logit_difference"), sem("logit_exp")
        s_pick, s_gate, s_gTp, s_gT = sem("picks_ready"), sem("gates_ready"), sem("gateT_in_psum"), sem("gateT_ready")
        s_up, s_gelu, s_dn, s_mix = sem("up_in_psum"), sem("hidden_ready"), sem("down_in_psum"), sem("mixed")
        s_out = sem("stored")

        def wait(eng, s, n):
            if not (isinstance(n, int) and n <= 0):
                eng.wait_ge(s, n)

        def pairs(eng, body):
            with eng.Fori(0, B // 2 - 1) as it:
                body(it * 2, 0)
                body(it * 2 + 1, 1)
            body(B - 2, 0)
            body(B - 1, 1)

        def sequences(eng, body):
            body(0)
            with eng.Fori(1, B - 1) as b:
                body(b)
            body(B - 1)

        N_W = 14
        N_SCR = 6
        N_LD = 6
        UP0, DN0, BK_T, BK_R = 0, 4, 6, 7
        BK_S, BK_A, BK_O, BK_M = 0, 4, 6, 7

        def e_tile(b, i):
            return b * NT + i

        block = ctx.enter_context(nc.Block())

        @block.sync
        def _(sp):
            sp.dma_start(x_sb[:, :, :], x.rearrange("(n p) c -> p n c", p=P)).then_inc(s_x, 16)
            for dst, src in ((id_sb, ident), (wq_sb, WqT), (wk_sb, WkT), (wv_sb, WvT), (iota_sb, iota8)):
                sp.dma_start(dst[:, :], src).then_inc(s_w, 16)
            for dst, src in ((bq_sb, bq), (bk_sb, bk)):
                sp.dma_start(dst[:, :], src.rearrange("(c o) -> c o", o=1)).then_inc(s_w, 16)
            for dst, src in ((bv_sb, bv), (bo_sb, bo)):
                sp.dma_start(dst[:, :], src.partition_broadcast(P)).then_inc(s_w, 16)
            for j in range(J):
                m = head_mask.rearrange("(g j) -> j g", j=J)[j, :].partition_broadcast(32)
                with nc.allow_non_contiguous_dma(reason="16 values"):
                    sp.dma_start(mask_sb[32 * j:32 * j + 32, :], m).then_inc(s_w, 16)
            sp.dma_start(wr_sb[:, :], Wr).then_inc(s_w, 16)
            sp.wait_ge(s_pad, 2)
            for j in range(J):
                src = WoT.rearrange("(g j d) n -> j d g n", g=HG, j=J)[j]
                sp.dma_start(wo_sb[32 * j + 1:32 * j + 1 + D, :, :], src).then_inc(s_wffn, 16)
            sp.dma_start(b2_sb[0:NE, :], b2).then_inc(s_wffn, 16)
            sp.dma_start(w1_sb[:, :, :], W1).then_inc(s_wffn, 16)
            sp.dma_start(b1_sb[:, :, :], b1).then_inc(s_wffn, 16)
            sp.dma_start(w2_sb[:, :, :, :], W2).then_inc(s_wffn, 16)

            def store_parts(b, par):
                sp.wait_ge(s_mid, 2 * b + 2)
                sp.wait_ge(s_lo, 2 * b + 2)
                sp.dma_start(q_scr[b, :, :], parts[:, par, 0, :, :]).then_inc(s_scr[par], 16)
                for r in range(PARTS):
                    for lo, hi, at in ((r, PARTS, 0), (0, r, PARTS - r)):
                        if hi > lo:
                            sp.dma_start(k_scr[r][b, :, at * S:(at + hi - lo) * S],
                                         parts[:, par, 1, lo:hi, :]).then_inc(s_scr[par], 16)

            pairs(sp, store_parts)
            for par in range(2):
                sp.wait_ge(s_scr[par], (B // 2) * (16 * N_SCR))

            def load_group(b, hg):
                wait(sp, s_sb, (b * HG + hg - HG + 1) * (2 * J))
                for r in range(PARTS):
                    for scr, op in ((q_scr, q_op), (k_scr[r], k_op)):
                        src = scr[b, J * D * hg:J * D * (hg + 1), :]
                        src = src.rearrange("(h d) (a t) -> (d a) h t", d=D, a=PARTS)
                        sp.dma_start(op[hg][PR * r:PR * (r + 1), :, :], src).then_inc(s_ld[hg], 16)

            def load_shift(b, hg):
                g = b * HG + hg
                sp.wait_ge(s_mxT, g + 1)
                for a in range(PARTS):
                    n = J * NT
                    sp.dma_start(q_op[hg][KR + a:KR + a + 1, :, :].rearrange("o j (n t) -> o (j n) t", t=P),
                                 mxT[n * a:n * (a + 1), hg % 2, :]).then_inc(s_sh[hg], 16)

            sp.wait_ge(s_const, 1)
            for hg in range(HG - 1):
                load_group(0, hg)
            load_shift(0, 0)

            def feed(b):
                last = isinstance(b, int) and b == B - 1
                for hg in range(HG):
                    if hg == 0:
                        load_group(b, HG - 1)
                    elif not last:
                        load_group(b + 1, hg - 1)
                    if hg < HG - 1:
                        load_shift(b, hg + 1)
                    elif not last:
                        load_shift(b + 1, 0)

            sequences(sp, feed)

            def store(b, par):
                sp.wait_ge(s_mix, (b + 1) * NE)
                sp.dma_start(out.rearrange("(n p) c -> p n c", p=P)[:, bass.ds(b * NT, NT), :],
                             x_sb[:, bass.ds(b * NT, NT), :]).then_inc(s_out, 16)

            pairs(sp, store)
            sp.wait_ge(s_out, 16 * B)

        @block.gpsimd
        def _(pool):
            nc.gpsimd.memset(wo_sb[:, :, :], 0.0).then_inc(s_pad, 1)
            nc.gpsimd.memset(b2_sb[:, :], 0.0).then_inc(s_pad, 1)
            nc.gpsimd.memset(neg_half[:, :], -0.5).then_inc(s_pad, 1)
            nc.gpsimd.memset(e_const[:, :], 2.718281828459045).then_inc(s_pad, 1)
            nc.gpsimd.memset(v_op[:, :, :, :, :], 0.0).then_inc(s_pad, 1)
            pool.wait_ge(s_pad, 5)
            nc.gpsimd.memset(v_op[:, :, :, :, 0:1], 1.0).then_inc(s_pad, 1)
            nc.gpsimd.memset(gate[:, :, :, :], 0.0).then_inc(s_pad, 1)
            pool.wait_ge(s_pad, 7)
            nc.gpsimd.memset(gate[:, :, :, E:E + 1], 1.0).then_inc(s_pad, 1)
            pool.wait_ge(s_pad, 8)
            pool.wait_ge(s_ve, 1)
            nc.gpsimd.tensor_tensor(rstd[:, :], var_eps[:, :], neg_half[:, :], ALU.pow).then_inc(s_rstd, 1)
            pool.wait_ge(s_v, B)

            def gather_v(b):
                for hg in range(HG):
                    wait(pool, s_pv, 2 * (b * HG + hg - HG + 1))
                    src = v_all[:, b, :, J * D * hg:J * D * (hg + 1)].rearrange("p n (j d) -> p n j d", j=J)
                    nc.gpsimd.tensor_copy(v_op[:, hg, :, :, 1:1 + D], src).then_inc(s_vop, 1)

            sequences(pool, gather_v)

            def ln2_and_router(b):
                pool.wait_ge(s_yve, b + 1)
                nc.gpsimd.tensor_tensor(y_rstd[:, :], var_eps[:, 0:NT], neg_half[:, 0:NT], ALU.pow).then_inc(s_yrs, 1)
                pool.wait_ge(s_gd, b + 1)
                nc.gpsimd.tensor_tensor(l_exp[:, :], e_const[:, :], l_diff[:, :], ALU.pow).then_inc(s_ge, 1)

            with pool.Fori(0, B) as b:
                ln2_and_router(b)

        @block.scalar
        def _(act):
            act.wait_ge(s_w, 16 * N_W)

            def project(b, par, it):
                act.wait_ge(s_xnTp, b + 1)
                nc.scalar.activation(xnT[:, par, :], ps[:, par, :], ACT.Copy).then_inc(s_xnT, 1)
                for w, (ready, bias) in enumerate(((s_qp, bq_sb), (s_kp, bk_sb))):
                    act.wait_ge(ready, b + 1)
                    wait(act, s_lo, 2 * (b - 1))
                    wait(act, s_scr[par], it * (16 * N_SCR))
                    nc.scalar.activation(qk32[:, par, w, :], ps[:, 2 + 2 * w + par, :], ACT.Identity,
                                         bias=bias[:, 0:1]).then_inc(s_qk32, 1)
                    act.wait_ge(s_qk32, 2 * b + w + 1)
                    nc.scalar.activation(parts[:, par, w, 0, :], qk32[:, par, w, :], ACT.Copy).then_inc(s_hi, 1)
                for w in range(2):
                    act.wait_ge(s_rest, 2 * b + w + 1)
                    nc.scalar.activation(parts[:, par, w, 1, :], rest[:, w, :], ACT.Copy).then_inc(s_mid, 1)

            project(0, 0, 0)
            project(1, 1, 0)
            with act.Fori(1, B // 2) as it:
                project(it * 2, 0, it)
                project(it * 2 + 1, 1, it)

            def exps(b):
                for hg in range(HG):
                    g = b * HG + hg
                    for half in range(2):
                        wait(act, s_pv, 2 * g + half - 1)
                        for j in range(J):
                            n = g * (2 * J) + half * J + j
                            act.wait_ge(s_sb, n + 1)
                            bank = BK_S + 2 * (j % 2)
                            nc.scalar.activation(probs[:, half, j, :], ps[:, bank:bank + 2, :].rearrange("p a t -> p (a t)"),
                                                 ACT.Exp, scale=float(D) ** -0.5).then_inc(s_exp, 1)

            sequences(act, exps)

            act.wait_ge(s_wffn, 16 * 8)
            act.wait_ge(s_pv, 2 * NG)

            def copy_yT(b, par):
                act.wait_ge(s_yTp, b + 1)
                nc.scalar.activation(yT[:, par, :], ps[:, BK_T, :], ACT.Copy).then_inc(s_yT, 1)

            def gelus(b, par):
                last = isinstance(b, int) and b == B - 1
                for e in range(NE):
                    n = b * NE + e
                    npar = (NE * par + e) % 2
                    for c in range(FC):
                        act.wait_ge(s_up, n * FC + c + 1)
                        if c == 0:
                            wait(act, s_dn, n - 1)
                        nc.scalar.activation(hid[:, npar, c, :], ps[:, UP0 + c, :], ACT.Gelu_apprx_tanh,
                                             bias=b1_sb[:, e, c:c + 1]).then_inc(s_gelu, 1)
                    if e == 4 and not last:
                        copy_yT(b + 1, 1 - par)

            copy_yT(0, 0)
            gelus(0, 0)
            gelus(1, 1)
            with act.Fori(1, B // 2 - 1) as it:
                gelus(it * 2, 0)
                gelus(it * 2 + 1, 1)
            gelus(B - 2, 0)
            gelus(B - 1, 1)

        @block.vector
        def _(dve):
            for hg in range(HG):
                last = nc.vector.memset(k_op[hg][64:SR, :, :], -1.0)
            last.then_inc(s_const, 1)
            nc.vector.memset(mx_parts[:, :], 0.0).then_inc(s_idbf, 1)
            dve.wait_ge(s_w, 16 * N_W)
            nc.vector.tensor_copy(id_bf[:, :], id_sb[:, :]).then_inc(s_idbf, 1)
            dve.wait_ge(s_x, 16)

            def moments(n, steps, at, ready):
                even, odd = stats[:, 0:n, 0:3], stats[:, 0:n, 3:6]
                dve.wait_ge(steps, at)
                nc.vector.tensor_tensor(mean_d[:, 0:n], even[:, :, 1], odd[:, :, 1], ALU.subtract).then_inc(steps, 1)
                nc.vector.tensor_tensor(mean[:, 0:n], even[:, :, 1], odd[:, :, 1], ALU.add).then_inc(steps, 1)
                nc.vector.tensor_tensor(dev[:, 0:n], even[:, :, 2], odd[:, :, 2], ALU.add).then_inc(steps, 1)
                dve.wait_ge(steps, at + 3)
                nc.vector.tensor_tensor(mean_d2[:, 0:n], mean_d[:, 0:n], mean_d[:, 0:n], ALU.mult).then_inc(steps, 1)
                nc.vector.tensor_scalar(mean[:, 0:n], mean[:, 0:n], 0.5, None, ALU.mult).then_inc(steps, 1)
                nc.vector.tensor_scalar(dev[:, 0:n], dev[:, 0:n], 1.0 / C, EPS, ALU.mult, ALU.add).then_inc(steps, 1)
                dve.wait_ge(steps, at + 6)
                nc.vector.scalar_tensor_tensor(out=var_eps[:, 0:n], in0=mean_d2[:, 0:n], scalar=0.25, in1=dev[:, 0:n],
                                               op0=ALU.mult, op1=ALU.add).then_inc(ready, 1)

            with dve.Fori(0, B) as b:
                for i in range(NT):
                    t = e_tile(b, i)
                    last = nc.vector.bn_stats(stats[:, t, :], x_sb[:, t, :])
                last.then_inc(s_st, 1)
            moments(B * NT, s_st, B, s_ve)
            dve.wait_ge(s_rstd, 1)

            def normalise(b, par):
                wait(dve, s_xnTp, b - 1)
                for i in range(NT):
                    t = e_tile(b, i)
                    last = nc.vector.tensor_scalar(xn[:, par, i, :], x_sb[:, t, :], mean[:, bass.ds(t, 1)], rstd[:, bass.ds(t, 1)],
                                                   ALU.subtract, ALU.mult)
                last.then_inc(s_xn, 1)

            def split(b, par):
                dve.wait_ge(s_vp, b + 1)
                nc.vector.tensor_tensor(v_all[:, b, :, :], ps[:, 6 + par, :].rearrange("p (n c) -> p n c", c=C),
                                        bv_sb[:, :].unsqueeze(1).to_broadcast([P, NT, C]), ALU.add).then_inc(s_v, 1)
                for w in range(2):
                    dve.wait_ge(s_hi, 2 * b + w + 1)
                    wait(dve, s_lo, 2 * b + w - 1)
                    nc.vector.tensor_tensor(rest[:, w, :], qk32[:, par, w, :], parts[:, par, w, 0, :],
                                            ALU.subtract).then_inc(s_rest, 1)
                for w in range(2):
                    dve.wait_ge(s_mid, 2 * b + w + 1)
                    nc.vector.tensor_tensor(parts[:, par, w, 2, :], rest[:, w, :], parts[:, par, w, 1, :],
                                            ALU.subtract).then_inc(s_lo, 1)

            normalise(0, 0)
            normalise(1, 1)
            split(0, 0)
            with dve.Fori(1, B // 2) as it:
                normalise(it * 2, 0)
                split(it * 2 - 1, 1)
                normalise(it * 2 + 1, 1)
                split(it * 2, 0)
            split(B - 1, 1)

            def row_max(g, a, slot):
                n = g * (J * NT) + a
                dve.wait_ge(s_sa, n + 1)
                nc.vector.reduce_max(mx[:, slot % 2, a:a + 1], ps[:, BK_A + a % 2, :], AX.X).then_inc(s_max, 1)

            def max_split(g, slot, step):
                m = mx[:, slot % 2, :]
                if step == 0:
                    dve.wait_ge(s_max, (g + 1) * (J * NT))
                    wait(dve, s_mxTp, g)
                    nc.vector.tensor_copy(mx_parts[:, 0:J * NT], m).then_inc(s_ms, 1)
                elif step == 1:
                    dve.wait_ge(s_ms, g * 3 + 1)
                    nc.vector.tensor_tensor(mx_rest[:, :], m, mx_parts[:, 0:J * NT], ALU.subtract).then_inc(s_ms, 1)
                elif step == 2:
                    dve.wait_ge(s_ms, g * 3 + 2)
                    nc.vector.tensor_copy(mx_parts[:, J * NT:2 * J * NT], mx_rest[:, :]).then_inc(s_ms, 1)
                else:
                    dve.wait_ge(s_ms, g * 3 + 3)
                    nc.vector.tensor_tensor(mx_parts[:, 2 * J * NT:3 * J * NT], mx_rest[:, :], mx_parts[:, J * NT:2 * J * NT],
                                            ALU.subtract).then_inc(s_msp, 1)

            def max_out(b, hg):
                g = b * HG + hg
                dve.wait_ge(s_mxTp, g + 1)
                if hg >= 2:
                    dve.wait_ge(s_sh[hg - 2], (b + 1) * (16 * PARTS))
                else:
                    wait(dve, s_sh[hg + 2], b * (16 * PARTS))
                nc.vector.tensor_copy(mxT[:, hg % 2, :], ps[0:PARTS * J * NT, BK_M, 0:P // 2].bitcast(bf16)).then_inc(s_mxT, 1)

            def out_norm(b, hg, step):
                g = b * HG + hg
                if step == 0:
                    wait(dve, s_o, g)
                    dve.wait_ge(s_pv, 2 * g + 2)
                    nc.vector.transpose(o_t[:, :, :].rearrange("p a c -> p (a c)"), ps[:, BK_O, :]).then_inc(s_ot, 1)
                elif step == 1:
                    dve.wait_ge(s_ot, g + 1)
                    nc.vector.reciprocal(o_rec[:, :], o_t[:, :, 0]).then_inc(s_orec, 1)
                elif step == 2:
                    dve.wait_ge(s_orec, g + 1)
                    nc.vector.scalar_tensor_tensor(out=o_t[:, :, 1:1 + D], in0=o_t[:, :, 1:1 + D],
                                                   scalar=mask_sb[:, hg:hg + 1],
                                                   in1=o_rec[:, :].unsqueeze(2).to_broadcast([P, S // 32, D]),
                                                   op0=ALU.mult, op1=ALU.mult).then_inc(s_onrm, 1)
                else:
                    dve.wait_ge(s_onrm, g + 1)
                    if hg == 0:
                        wait(dve, s_ap, b)
                    nc.vector.transpose(o_sb[:, hg, :], o_t[:, :, :].rearrange("p a c -> p (a c)")).then_inc(s_o, 1)

            def residual(b):
                dve.wait_ge(s_ap, b + 1)
                sl = x_sb[:, bass.ds(b * NT, NT), :]
                nc.vector.tensor_tensor(sl, ps[:, BK_M, :].rearrange("p (n c) -> p n c", c=C), sl, ALU.add).then_inc(s_x2, 1)

            with dve.Fori(0, B) as b:
                sl = x_sb[:, bass.ds(b * NT, NT), :]
                nc.vector.tensor_tensor(sl, sl, bo_sb[:, :].unsqueeze(1).to_broadcast([P, NT, C]), ALU.add).then_inc(s_xbo, 1)
            dve.wait_ge(s_xbo, B)

            for a in range(J * NT):
                row_max(0, a, 0)
            for a in range(J * NT):
                row_max(1, a, 1)
                if a < 4:
                    max_split(0, 0, a)
                if a == 8:
                    max_out(0, 0)

            def attend(b):
                first, last = isinstance(b, int) and b == 0, isinstance(b, int) and b == B - 1
                for hg in range(HG):
                    g = b * HG + hg
                    ahead = not last or hg < HG - 2
                    nxt = not last or hg < HG - 1
                    for a in range(J * NT):
                        if ahead:
                            row_max(g + 2, a, hg)
                        if nxt and a < 4:
                            max_split(g + 1, hg + 1, a)
                        if a == 6 and hg == 1 and not first:
                            residual(b - 1)
                        if nxt and a == 9:
                            if hg < HG - 1:
                                max_out(b, hg + 1)
                            else:
                                max_out(b + 1, 0)
                        if 10 <= a < 14:
                            if hg > 0:
                                out_norm(b, hg - 1, a - 10)
                            elif not first:
                                out_norm(b - 1, HG - 1, a - 10)

            sequences(dve, attend)
            for step in range(4):
                out_norm(B - 1, HG - 1, step)
            residual(B - 1)

            def ln2_moments(b):
                dve.wait_ge(s_x2, b + 1)
                for i in range(NT):
                    last = nc.vector.bn_stats(stats[:, i, :], x_sb[:, e_tile(b, i), :])
                last.then_inc(s_yst, 1)
                moments(NT, s_yst, b * 7 + 1, s_yve)

            def ln2_normalise(b, par):
                dve.wait_ge(s_yrs, b + 1)
                wait(dve, s_yTp, b - 1)
                for i in range(NT):
                    last = nc.vector.tensor_scalar(y[:, par, i, :], x_sb[:, e_tile(b, i), :], mean[:, i:i + 1],
                                                   y_rstd[:, i:i + 1], ALU.subtract, ALU.mult)
                last.then_inc(s_y, 1)

            R = 7

            def router_top(b):
                dve.wait_ge(s_lgp, b + 1)
                nc.vector.tensor_copy(logits[:, :, :], ps[:, BK_R, 0:NT * E].rearrange("p (n e) -> p n e", e=E)).then_inc(s_rt, 1)
                dve.wait_ge(s_rt, b * R + 1)
                nc.vector.reduce_max(top1[:, :], logits[:, :, :], AX.X)
                for i in range(NT):
                    last = nc.vector.max(top8[:, i, :], logits[:, i, :])
                last.then_inc(s_rt, 1)
                dve.wait_ge(s_rt, b * R + 2)
                nc.vector.tensor_tensor(l_diff[:, :], top8[:, :, 1], top1[:, :], ALU.subtract).then_inc(s_gd, 1)
                for i in range(NT):
                    last = nc.vector.max_index(top_i[:, i, :], top8[:, i, :], logits[:, i, :])
                last.then_inc(s_rt, 1)
                dve.wait_ge(s_rt, b * R + 3)
                nc.vector.tensor_copy(top_if[:, :, :], top_i[:, :, 0:2]).then_inc(s_rt, 1)

            def router_gates(b, par):
                dve.wait_ge(s_ge, b + 1)
                nc.vector.tensor_scalar(l_sum[:, :], l_exp[:, :], 1.0, None, ALU.add).then_inc(s_rt, 1)
                dve.wait_ge(s_rt, b * R + 5)
                nc.vector.reciprocal(top_p[:, 0, :], l_sum[:, :]).then_inc(s_rt, 1)
                dve.wait_ge(s_rt, b * R + 6)
                nc.vector.tensor_tensor(top_p[:, 1, :], l_exp[:, :], top_p[:, 0, :], ALU.mult).then_inc(s_rt, 1)
                dve.wait_ge(s_rt, b * R + 7)
                for k in range(2):
                    for i in range(NT):
                        last = nc.vector.tensor_scalar(pick[:, k, i, :], iota_sb[:, :], top_if[:, i, k:k + 1],
                                                       top_p[:, k, i:i + 1], ALU.is_equal, ALU.mult)
                last.then_inc(s_pick, 1)
                dve.wait_ge(s_pick, b + 1)
                nc.vector.tensor_tensor(gate[:, par, :, 0:E], pick[:, 0, :, :], pick[:, 1, :, :], ALU.add).then_inc(s_gate, 1)

            def gates_out(b, par):
                dve.wait_ge(s_gTp, b + 1)
                nc.vector.tensor_copy(gateT[:, par, :], ps[:, BK_T, :]).then_inc(s_gT, 1)

            def mix(b, par, e):
                n = b * NE + e
                bank = DN0 + (NE * par + e) % 2
                dve.wait_ge(s_dn, n + 1)
                wait(dve, s_mix, n)
                if e < E:
                    for i in range(NT):
                        t = e_tile(b, i)
                        last = nc.vector.scalar_tensor_tensor(
                            out=x_sb[:, t, :], in0=ps[:, bank, C * i:C * (i + 1)], scalar=gate[:, par, i, e:e + 1],
                            in1=x_sb[:, t, :], op0=ALU.mult, op1=ALU.add)
                    last.then_inc(s_mix, 1)
                else:
                    sl = x_sb[:, bass.ds(b * NT, NT), :]
                    nc.vector.tensor_tensor(sl, ps[:, bank, :].rearrange("p (n c) -> p n c", c=C), sl, ALU.add).then_inc(s_mix, 1)

            def mixture(b, par):
                last = isinstance(b, int) and b == B - 1
                dve.wait_ge(s_gate, b + 1)
                for e in range(NE):
                    mix(b, par, e)
                    if not last:
                        if e == 0:
                            ln2_moments(b + 1)
                        if e == 2:
                            ln2_normalise(b + 1, 1 - par)
                        if e == 5:
                            router_top(b + 1)
                        if e == 6:
                            router_gates(b + 1, 1 - par)
                        if e == 7:
                            gates_out(b + 1, 1 - par)

            ln2_moments(0)
            ln2_normalise(0, 0)
            router_top(0)
            router_gates(0, 0)
            gates_out(0, 0)
            mixture(0, 0)
            mixture(1, 1)
            with dve.Fori(1, B // 2 - 1) as it:
                mixture(it * 2, 0)
                mixture(it * 2 + 1, 1)
            mixture(B - 2, 0)
            mixture(B - 1, 1)

        @block.tensor
        def _(pe):
            pe.wait_ge(s_w, 16 * N_W)
            pe.wait_ge(s_idbf, 2)

            def project(b, par):
                pe.wait_ge(s_xn, b + 1)
                wait(pe, s_xnT, b - 1)
                for i in range(NT):
                    last = nc.tensor.transpose(ps[:, par, P * i:P * (i + 1)], xn[:, par, i, :], id_sb[:, :])
                last.then_inc(s_xnTp, 1)
                pe.wait_ge(s_xnT, b + 1)
                wait(pe, s_qk32, 2 * (b - 1))
                nc.tensor.matmul(ps[:, 2 + par, :], wq_sb[:, :], xnT[:, par, :], start=True, stop=True).then_inc(s_qp, 1)
                nc.tensor.matmul(ps[:, 4 + par, :], wk_sb[:, :], xnT[:, par, :], start=True, stop=True).then_inc(s_kp, 1)
                wait(pe, s_v, b - 1)
                for i in range(NT):
                    last = nc.tensor.matmul(ps[:, 6 + par, C * i:C * (i + 1)], xnT[:, par, P * i:P * (i + 1)], wv_sb[:, :],
                                            start=True, stop=True)
                last.then_inc(s_vp, 1)

            project(0, 0)
            project(1, 1)
            with pe.Fori(1, B // 2) as it:
                project(it * 2, 0)
                project(it * 2 + 1, 1)

            pe.wait_ge(s_xnT, B)
            pe.wait_ge(s_qk32, 2 * B)
            pe.wait_ge(s_v, B)

            def row_scores(b, hg, a):
                n = (b * HG + hg) * (J * NT) + a
                j, i = a // NT, a % NT
                if a == 0:
                    pe.wait_ge(s_ld[hg], (b + 1) * (16 * N_LD))
                wait(pe, s_max, n - 1)
                nc.tensor.matmul(ps[:, BK_A + a % 2, :], q_op[hg][0:KR, j, P * i:P * (i + 1)], k_op[hg][0:KR, j, :],
                                 start=True, stop=True).then_inc(s_sa, 1)

            def key_scores(b, hg, half, j):
                n = (b * HG + hg) * (2 * J) + half * J + j
                if half == 0 and j == 0:
                    pe.wait_ge(s_sh[hg], (b + 1) * (16 * PARTS))
                wait(pe, s_exp, n - 1)
                for kk in range(2):
                    i = 2 * half + kk
                    last = nc.tensor.matmul(ps[:, BK_S + 2 * (j % 2) + kk, :], k_op[hg][:, j, P * i:P * (i + 1)],
                                            q_op[hg][:, j, :], start=True, stop=True)
                last.then_inc(s_sb, 1)

            def pv(b, hg, half):
                g = b * HG + hg
                pe.wait_ge(s_exp, g * (2 * J) + (half + 1) * J)
                if half == 0:
                    wait(pe, s_ot, g)
                    pe.wait_ge(s_vop, g + 1)
                for kk in range(2):
                    i = 2 * half + kk
                    for j in range(J):
                        last = nc.tensor.matmul(ps[32 * j:32 * j + 32, BK_O, :], v_op[:, hg, i, j, :],
                                                probs[:, half, j, S * kk:S * (kk + 1)], start=(i == 0), stop=(i == NT - 1))
                last.then_inc(s_pv, 1)

            def max_rows(b, hg):
                g = b * HG + hg
                pe.wait_ge(s_msp, g + 1)
                wait(pe, s_mxT, g)
                if hg == 2:
                    wait(pe, s_x2, b)
                nc.tensor.transpose(ps[:, BK_M, 0:P // 2].bitcast(bf16), mx_parts[:, :], id_bf[:, :]).then_inc(s_mxTp, 1)

            def project_out(b):
                pe.wait_ge(s_o, HG * (b + 1))
                last_b = isinstance(b, int) and b == B - 1
                pe.wait_ge(s_mxT, NG if last_b else (b + 1) * HG + 2)
                for i in range(NT):
                    for hg in range(HG):
                        last = nc.tensor.matmul(ps[:, BK_M, C * i:C * (i + 1)], o_sb[:, hg, P * i:P * (i + 1)], wo_sb[:, hg, :],
                                                start=(hg == 0), stop=(hg == HG - 1))
                last.then_inc(s_ap, 1)

            for hg in range(2):
                for a in range(J * NT):
                    row_scores(0, hg, a)
                    if hg == 1 and a == 6:
                        max_rows(0, 0)

            def attend(b):
                first, last_b = isinstance(b, int) and b == 0, isinstance(b, int) and b == B - 1
                for hg in range(HG):
                    for half in range(2):
                        for j in range(J):
                            key_scores(b, hg, half, j)
                            for a in (8 * half + 2 * j, 8 * half + 2 * j + 1):
                                if hg < HG - 2:
                                    row_scores(b, hg + 2, a)
                                elif not last_b:
                                    row_scores(b + 1, hg - 2, a)
                            if half == 1 and j == 0:
                                if hg < HG - 1:
                                    max_rows(b, hg + 1)
                                elif not last_b:
                                    max_rows(b + 1, 0)
                            if half == 0 and j == 0 and hg == 1 and not first:
                                pe.wait_ge(s_wffn, 16 * 8)
                                project_out(b - 1)
                            if j == 2:
                                if half == 1:
                                    pv(b, hg, 0)
                                elif hg > 0:
                                    pv(b, hg - 1, 1)
                                elif not first:
                                    pv(b - 1, HG - 1, 1)

            sequences(pe, attend)
            pv(B - 1, HG - 1, 1)
            project_out(B - 1)

            pe.wait_ge(s_exp, NG * 2 * J)
            pe.wait_ge(s_max, NG * J * NT)
            pe.wait_ge(s_ot, NG)

            def transpose_y(b, par):
                pe.wait_ge(s_y, b + 1)
                wait(pe, s_gT, b)
                for i in range(NT):
                    last = nc.tensor.transpose(ps[:, BK_T, P * i:P * (i + 1)], y[:, par, i, :], id_sb[:, :])
                last.then_inc(s_yTp, 1)

            def router(b, par):
                pe.wait_ge(s_yT, b + 1)
                wait(pe, s_rt, b * 7 - 6)
                if isinstance(b, int) and b == 0:
                    pe.wait_ge(s_x2, B)
                for i in range(NT):
                    last = nc.tensor.matmul(ps[:, BK_R, E * i:E * (i + 1)], yT[:, par, P * i:P * (i + 1)], wr_sb[:, :],
                                            start=True, stop=True)
                last.then_inc(s_lgp, 1)

            def transpose_gates(b, par):
                pe.wait_ge(s_gate, b + 1)
                for i in range(NT):
                    last = nc.tensor.transpose(ps[:, BK_T, P * i:P * (i + 1)], gate[:, par, i, :], id_sb[:, :])
                last.then_inc(s_gTp, 1)

            def up(b, par, e):
                n = b * NE + e
                pe.wait_ge(s_yT, b + 1)
                for c in range(FC):
                    wait(pe, s_gelu, (n - 1) * FC + c + 1)
                    nc.tensor.matmul(ps[:, UP0 + c, :], w1_sb[:, e, P * c:P * (c + 1)], yT[:, par, :],
                                     start=True, stop=True).then_inc(s_up, 1)

            def down(b, par, e):
                n = b * NE + e
                npar = (NE * par + e) % 2
                pe.wait_ge(s_gelu, (n + 1) * FC)
                wait(pe, s_mix, n - 1)
                if e == E:
                    pe.wait_ge(s_gT, b + 1)
                for i in range(NT):
                    for c in range(FC):
                        last = nc.tensor.matmul(ps[:, DN0 + npar, C * i:C * (i + 1)], hid[:, npar, c, P * i:P * (i + 1)],
                                                w2_sb[:, e, c, :], start=(c == 0), stop=(c == FC - 1 and e < E))
                    if e == E:
                        last = nc.tensor.matmul(ps[:, DN0 + npar, C * i:C * (i + 1)], gateT[:, par, P * i:P * (i + 1)],
                                                b2_sb[:, :], start=False, stop=True)
                last.then_inc(s_dn, 1)

            def mixture(b, par):
                last_b = isinstance(b, int) and b == B - 1
                for e in range(NE):
                    if e < E:
                        up(b, par, e + 1)
                    elif not last_b:
                        up(b + 1, 1 - par, 0)
                    down(b, par, e)
                    if not last_b:
                        if e == 3:
                            transpose_y(b + 1, 1 - par)
                        if e == 4:
                            router(b + 1, 1 - par)
                        if e == 6:
                            transpose_gates(b + 1, 1 - par)

            transpose_y(0, 0)
            router(0, 0)
            up(0, 0, 0)
            transpose_gates(0, 0)
            mixture(0, 0)
            mixture(1, 1)
            with pe.Fori(1, B // 2 - 1) as it:
                mixture(it * 2, 0)
                mixture(it * 2 + 1, 1)
            mixture(B - 2, 0)
            mixture(B - 1, 1)


def kernel(**a):
    import numpy as np
    import concourse.bacc as bacc
    from concourse import mybir as mb
    from concourse.bass_utils import run_bass_kernel_spmd as run

    a = {k.replace("L0_attn_", "a_").replace("L0_ffn_", "f_"): np.asarray(v) for k, v in a.items()}
    with_shared = lambda routed, shared: np.concatenate([routed, shared[None]], axis=0)
    ins = {
        "x": a["a_x"].reshape(B * S, C),
        "WqT": a["a_Wq"].T, "WkT": a["a_Wk"].T, "WvT": a["a_Wv"].T, "WoT": a["a_Wo"].T,
        "bq": a["a_bq"], "bk": a["a_bk"], "bv": a["a_bv"], "bo": a["a_bo"], "head_mask": a["a_head_mask"],
        "W1": with_shared(a["f_Wfc"], a["f_Wfc_s"]).transpose(1, 0, 2),
        "b1": with_shared(a["f_bfc"], a["f_bfc_s"]).reshape(NE, FC, P).transpose(2, 0, 1),
        "W2": with_shared(a["f_Wproj"], a["f_Wproj_s"]).reshape(NE, FC, P, C).transpose(2, 0, 1, 3),
        "b2": with_shared(a["f_bproj"], a["f_bproj_s"]),
        "Wr": a["f_Wr"],
        "ident": np.eye(P, dtype=np.float32),
        "iota8": np.tile(np.arange(E, dtype=np.float32), (P, 1)),
    }
    nc = bacc.Bacc("TRN2", target_bir_lowering=False, num_devices=1)
    arrays, aps = {}, {}
    for name, v in ins.items():
        v = np.ascontiguousarray(v)
        arrays[f"in_{name}"] = v
        aps[name] = nc.dram_tensor(f"in_{name}", v.shape, mb.dt.from_np(v.dtype), kind="ExternalInput").ap()
    aps["out"] = nc.dram_tensor("out_0", (B * S, C), mb.dt.float32, kind="ExternalOutput").ap()
    block_kernel(nc, **aps)
    r = run(nc, [arrays], core_ids=[0])
    return r.results[0]["out_0"].reshape(B, S, C)
```

```python
import concourse.bass as bass
from concourse import mybir
from contextlib import ExitStack

B, S, C = 8, 512, 128
H, D = 16, 8
J = 4
HG = H // J
P = 128
NT = S // P
PARTS = 3
PR = PARTS * D
KR = PARTS * PR
SH = 96
E, F = 8, 512
NE = E + 1
FC = F // P
EPS = 1e-5
NG = B * HG
K2 = 2
NC = NT * K2
TR = 256
TH = TR // P
TILES = K2 * B * S // TR + E
REGION = B * S + TR
ROW = C + 1
RING = 4


def block_kernel(nc, x, WqT, WkT, WvT, WoT, bq, bk, bv, bo, head_mask, W1, b1, W2, b2, Wr, ident, iota8,
                 tri, region_at, row_ids, dump_ids, thresholds, tri8, tile_ids, region_row, out):
    f32, bf16, u32 = mybir.dt.float32, mybir.dt.bfloat16, mybir.dt.uint32
    ALU, ACT, AX = mybir.AluOpType, mybir.ActivationFunctionType, mybir.AxisListType

    q_scr = nc.dram_tensor("q_scr", (B, H * D, PARTS * S), bf16, kind="Internal").ap()
    k_scr = [nc.dram_tensor(f"k_scr{r}", (B, H * D, PARTS * S), bf16, kind="Internal").ap() for r in range(PARTS)]
    slots = nc.dram_tensor("slots", (E * REGION + E * TR, ROW), f32, kind="Internal").ap()
    results = nc.dram_tensor("results", (K2 * B * S + K2 * E * TR, C), f32, kind="Internal").ap()

    ctx = ExitStack()
    with ctx:
        def sb(name, shape, dt=f32):
            return ctx.enter_context(nc.sbuf_tensor(name, shape, dt))

        def sem(name):
            return ctx.enter_context(nc.semaphore(name))

        wq_sb, wk_sb, wv_sb = sb("wq_sb", [P, C]), sb("wk_sb", [P, C]), sb("wv_sb", [P, C])
        wo_sb = sb("wo_sb", [P, HG, C])
        bq_sb, bk_sb = sb("bq_sb", [P, 1]), sb("bk_sb", [P, 1])
        bv_sb, bo_sb = sb("bv_sb", [P, C]), sb("bo_sb", [P, C])
        mask_sb = sb("mask_sb", [P, HG])
        w1_sb, b1_sb = sb("w1_sb", [P, NE, F]), sb("b1_sb", [P, NE, FC])
        w2_sb = sb("w2_sb", [P, NE, FC, C])
        b2_sb = sb("b2_sb", [P, NE, C])
        wr_sb = sb("wr_sb", [P, E])
        id_sb, id_bf = sb("id_sb", [P, P]), sb("id_bf", [P, P], bf16)
        iota_sb = sb("iota_sb", [P, E])
        neg_half, e_const = sb("neg_half", [P, B * NT]), sb("e_const", [P, B * NT])
        x_sb = sb("x_sb", [P, B * NT, C])
        stats = sb("stats", [P, B * NT, 6])
        mean, mean_d = sb("mean", [P, B * NT]), sb("mean_d", [P, B * NT])
        dev, mean_d2 = sb("dev", [P, B * NT]), sb("mean_d2", [P, B * NT])
        var_eps, rstd = sb("var_eps", [P, B * NT]), sb("rstd", [P, B * NT])
        xn = sb("xn", [P, 2, NT, C])
        xnT = sb("xnT", [P, 2, S])
        qk32 = sb("qk32", [P, 2, 2, S])
        rest = sb("rest", [P, 2, S])
        parts = sb("parts", [P, 2, 2, PARTS, S], bf16)
        v_all = sb("v_all", [P, B, NT, C])
        q_op = [sb(f"q_op{g}", [P, J, S], bf16) for g in range(HG)]
        k_op = [sb(f"k_op{g}", [P, J, S], bf16) for g in range(HG)]
        v_op = sb("v_op", [P, HG, NT, J, 32])
        mx = sb("mx", [P, 2, J * NT])
        mx_rest = sb("mx_rest", [P, J * NT])
        mx_parts = sb("mx_parts", [P, P], bf16)
        mxT = sb("mxT", [PARTS * J * NT, 2, P], bf16)
        probs = sb("probs", [P, NT, J, S])
        o_t = sb("o_t", [P, S // 32, 32])
        o_rec = sb("o_rec", [P, S // 32])
        o_sb = sb("o_sb", [P, HG, S])
        logits, top1, top8 = sb("logits", [P, NT, E]), sb("top1", [P, NT]), sb("top8", [P, NT, 8])
        top_i, top_if = sb("top_i", [P, NT, 8], u32), sb("top_if", [P, NT, 2])
        l_diff, l_exp = sb("l_diff", [P, B * NT]), sb("l_exp", [P, B * NT])
        l_sum, top_p = sb("l_sum", [P, B * NT]), sb("top_p", [P, K2, B * NT])
        ids_sb = sb("ids_sb", [P, B * NT, K2], u32)
        zero_sb = sb("zero_sb", [P, TH, C])
        dump_sb = sb("dump_sb", [P, K2 * E, TH, 1], u32)
        tri_f, tri_bf, ones_bf = sb("tri_f", [P, P]), sb("tri_bf", [P, P], bf16), sb("ones_bf", [P, P], bf16)
        reg_f, reg_bf = sb("reg_f", [P, E]), sb("reg_bf", [P, E], bf16)
        chosen = sb("chosen", [P, NC, E], bf16)
        seq_n = sb("seq_n", [P, E])
        run_n, run_bf = sb("run_n", [P, E]), sb("run_bf", [P, E], bf16)
        at_f, slot_f = sb("at_f", [P, NC, E]), sb("slot_f", [P, NC])
        slot_u = sb("slot_u", [P, NC], u32)
        thr_sb, tri8_sb, tid_sb, regr_sb = sb("thr_sb", [1, B * S // TR]), sb("tri8_sb", [1, E, E]), sb("tid_sb", [1, TILES]), sb("regr_sb", [1, E])
        cnt, n_tiles = sb("cnt", [1, E]), sb("n_tiles", [1, E])
        tile_end = sb("tile_end", [1, E])
        t_exp, t_first, t_row = sb("t_exp", [1, TILES]), sb("t_first", [1, TILES]), sb("t_row", [1, TILES])
        pad_f = sb("pad_f", [1, E])
        tab_e, tab_row, pad_row = sb("tab_e", [1, TILES], u32), sb("tab_row", [1, TILES], u32), sb("pad_row", [1, E], u32)
        b1_cur = sb("b1_cur", [P, 2, FC])
        row_id = sb("row_id", [P, 2, TH], u32)
        yT = v_all.rearrange("p b n c -> p b (n c)")
        yT_now = xnT[:, 0, :]
        in_parts = parts.rearrange("p a w k s -> p (a w k s)").bitcast(f32)
        at = [0]

        def place(rows, *shape):
            n, lo = 1, at[0]
            for d in shape:
                n *= d
            at[0] = lo + n
            return in_parts[0:rows, lo:lo + n]

        y2 = place(P, NT, K2, ROW).rearrange("p (n k c) -> p n k c", n=NT, k=K2)
        over = place(1, E, B * S // TR).rearrange("p (e n) -> p e n", e=E)
        upto = place(1, E, E).rearrange("p (e n) -> p e n", e=E)
        past = place(1, TILES, E).rearrange("p (t e) -> p t e", t=TILES)
        past_n = place(1, TILES, E).rearrange("p (t e) -> p t e", t=TILES)
        yT_tile = xn.rearrange("p a n c -> p (a n c)")[:, 0:2 * TR].rearrange("p (a t) -> p a t", a=2)
        r_tile = rest.rearrange("p a s -> p (a s)")[:, 0:2 * TH * C].rearrange("p (a h c) -> p a h c", a=2, h=TH)
        w1_cur = qk32[:, 0, :, :]
        w2_cur = qk32[:, 1, :, :].rearrange("p a (c n) -> p a c n", c=FC)
        hid = probs[:, 0:2, :, :]
        hid_tile = probs[:, 0, :, :].rearrange("p c s -> p (c s)").rearrange("p (a c t) -> p a c t", a=2, c=FC)
        r_ring = probs[:, 2:4, :, :].rearrange("p x y s -> p (x y s)").rearrange("p (u n k c) -> p u n k c", u=RING, n=NT, k=K2)
        y_tile = probs[:, 2, :, :].rearrange("p y s -> p (y s)")[:, 0:RING * TH * ROW].rearrange("p (u h c) -> p u h c", u=RING, h=TH)
        ps = ctx.enter_context(nc.psum_tensor("ps", [P, 8, 512], f32))

        s_x, s_w, s_wffn = sem("x_loaded"), sem("weights_loaded"), sem("ffn_weights_loaded")
        s_const, s_idbf, s_pad = sem("constants_set"), sem("id_bf_set"), sem("padding_set")
        s_st, s_ve, s_rstd = sem("ln_steps"), sem("ln_var_eps"), sem("ln_rstd")
        s_xn, s_xnTp, s_xnT = sem("xn_ready"), sem("xnT_in_psum"), sem("xnT_ready")
        s_qp, s_kp, s_vp = sem("q_in_psum"), sem("k_in_psum"), sem("v_in_psum")
        s_qk32, s_hi, s_rest = sem("qk32_ready"), sem("first_parts_ready"), sem("rest_ready")
        s_mid, s_lo, s_v, s_scr = sem("second_parts_ready"), sem("third_parts_ready"), sem("v_stored"), [sem("scratch_stored0"), sem("scratch_stored1")]
        s_ld = [sem(f"qk_op_loaded{g}") for g in range(HG)]
        s_sh = [sem(f"shift_rows_loaded{g}") for g in range(HG)]
        s_sa, s_max = sem("row_scores_in_psum"), sem("row_maxima_taken")
        s_ms, s_msp, s_mxTp, s_mxT = sem("max_split_steps"), sem("max_parts_ready"), sem("mxT_in_psum"), sem("mxT_ready")
        s_sb, s_exp = sem("key_scores_in_psum"), sem("probs_ready")
        s_vop, s_pv = sem("v_op_ready"), sem("pv_key_tiles_done")
        s_ot, s_orec, s_onrm, s_o = sem("o_transposed"), sem("o_reciprocal"), sem("o_normalised"), sem("o_ready")
        s_xbo, s_ap, s_x2 = sem("x_plus_bias"), sem("attention_projected"), sem("x2_ready")
        s_y, s_yTp, s_yT = sem("y_rows_ready"), sem("yT_in_psum"), sem("yT_ready")
        s_lgp, s_rt, s_gd, s_ge = sem("logits_in_psum"), sem("router_steps"), sem("logit_differences"), sem("logit_exps")
        s_sl, s_yn, s_bn = sem("slot_sums"), sem("y_ready"), sem("ln2_begun")
        s_rk, s_slot, s_tab = sem("ranks_in_psum"), sem("slots_ready"), sem("table_steps")
        s_put, s_fill, s_route = sem("slots_written"), sem("filling_written"), sem("routing_constants")
        s_up, s_gelu, s_dn, s_mix = sem("shared_up_in_psum"), sem("shared_hidden_ready"), sem("shared_down_in_psum"), sem("shared_added")
        s_yl = [sem(f"y_tile_loaded{u}") for u in range(RING)]
        s_tT, s_tyT, s_tup, s_th = sem("tile_T_in_psum"), sem("tile_yT_ready"), sem("tile_up_in_psum"), sem("tile_hidden_ready")
        s_tdn, s_w1c, s_w2c, s_rid = sem("tile_down_in_psum"), sem("tile_w1_ready"), sem("tile_w2_ready"), sem("tile_row_ids")
        s_rt2, s_res = sem("tile_result_ready"), [sem("results_written0"), sem("results_written1")]
        s_rl, s_gate, s_b2s, s_fin = [sem(f"results_loaded{u}") for u in range(RING)], sem("gate_steps"), sem("shared_bias_added"), sem("combined")
        s_part, s_cn, s_cntp = sem("first_choice_added"), sem("slot_steps"), sem("counts_in_psum")
        s_go, s_out = sem("scatter_steps"), sem("stored")

        def wait(eng, s, n):
            if not (isinstance(n, int) and n <= 0):
                eng.wait_ge(s, n)

        def pairs(eng, body):
            with eng.Fori(0, B // 2 - 1) as it:
                body(it * 2, 0)
                body(it * 2 + 1, 1)
            body(B - 2, 0)
            body(B - 1, 1)

        def sequences(eng, body):
            body(0)
            with eng.Fori(1, B - 1) as b:
                body(b)
            body(B - 1)

        N_W = 14
        N_SCR = 6
        N_ROUTE = 8
        N_LD = 6
        UP0, DN0 = 0, 4
        BK_TT, BK_TU, BK_TD = 0, 2, 6
        BK_S, BK_A, BK_O, BK_M = 0, 2, 6, 7

        PV_LAG, YT_STEP = 11, 11
        R, Q = 5, 3

        def e_tile(b, i):
            return b * NT + i

        N_MAT = 4
        N_TAB = N_MAT + 16

        block = ctx.enter_context(nc.Block())

        @block.sync
        def _(sp):
            sp.dma_start(x_sb[:, :, :], x.rearrange("(n p) c -> p n c", p=P)).then_inc(s_x, 16)
            for dst, src in ((id_sb, ident), (wq_sb, WqT), (wk_sb, WkT), (wv_sb, WvT), (iota_sb, iota8)):
                sp.dma_start(dst[:, :], src).then_inc(s_w, 16)
            for dst, src in ((bq_sb, bq), (bk_sb, bk)):
                sp.dma_start(dst[:, :], src.rearrange("(c o) -> c o", o=1)).then_inc(s_w, 16)
            for dst, src in ((bv_sb, bv), (bo_sb, bo)):
                sp.dma_start(dst[:, :], src.partition_broadcast(P)).then_inc(s_w, 16)
            for j in range(J):
                m = head_mask.rearrange("(g j) -> j g", j=J)[j, :].partition_broadcast(32)
                with nc.allow_non_contiguous_dma(reason="16 values"):
                    sp.dma_start(mask_sb[32 * j:32 * j + 32, :], m).then_inc(s_w, 16)
            sp.dma_start(wr_sb[:, :], Wr).then_inc(s_w, 16)
            sp.wait_ge(s_pad, 1)
            for j in range(J):
                src = WoT.rearrange("(g j d) n -> j d g n", g=HG, j=J)[j]
                sp.dma_start(wo_sb[32 * j + 1:32 * j + 1 + D, :, :], src).then_inc(s_wffn, 16)
            sp.dma_start(b2_sb[:, :, :], b2.partition_broadcast(P)).then_inc(s_wffn, 16)
            sp.dma_start(w1_sb[:, :, :], W1).then_inc(s_wffn, 16)
            sp.dma_start(b1_sb[:, :, :], b1).then_inc(s_wffn, 16)
            sp.dma_start(w2_sb[:, :, :, :], W2).then_inc(s_wffn, 16)
            for dst, src in ((tri_f, tri), (reg_f, region_at), (thr_sb, thresholds), (tid_sb, tile_ids), (regr_sb, region_row)):
                sp.dma_start(dst[:, :], src).then_inc(s_route, 16)
            sp.dma_start(tri8_sb[:, :, :], tri8).then_inc(s_route, 16)
            sp.dma_start(ids_sb[:, :, :], row_ids.rearrange("(n p) k -> p n k", p=P)).then_inc(s_route, 16)
            sp.wait_ge(s_pad, 2)
            sp.dma_start(dump_sb[:, :, :, :], dump_ids).then_inc(s_route, 16)
            sp.wait_ge(s_route, 16 * N_ROUTE)

            def fill(at, n):
                to = slots[bass.ds(at, TR), :].rearrange("(h p) c -> p h c", p=P)
                sp.dma_start(to[:, :, 0:C], zero_sb[:, :, :]).then_inc(s_fill, 16)
                with nc.allow_non_contiguous_dma(reason="256 row numbers"):
                    sp.dma_start(to[:, :, C:ROW].bitcast(u32), dump_sb[:, n, :, :]).then_inc(s_fill, 16)

            for n in range(E):
                fill(E * REGION + TR * n, E + n)

            def store_parts(b, par):
                sp.wait_ge(s_mid, 2 * b + 2)
                sp.wait_ge(s_lo, 2 * b + 2)
                sp.dma_start(q_scr[b, :, :], parts[:, par, 0, :, :]).then_inc(s_scr[par], 16)
                for r in range(PARTS):
                    for lo, hi, at in ((r, PARTS, 0), (0, r, PARTS - r)):
                        if hi > lo:
                            sp.dma_start(k_scr[r][b, :, at * S:(at + hi - lo) * S],
                                         parts[:, par, 1, lo:hi, :]).then_inc(s_scr[par], 16)

            pairs(sp, store_parts)
            for par in range(2):
                sp.wait_ge(s_scr[par], (B // 2) * (16 * N_SCR))

            def load_group(b, hg):
                wait(sp, s_sb, (b * HG + hg - HG + 1) * (J * NT))
                for r in range(PARTS):
                    for scr, op in ((q_scr, q_op), (k_scr[r], k_op)):
                        src = scr[b, J * D * hg:J * D * (hg + 1), :]
                        src = src.rearrange("(h d) (a t) -> (d a) h t", d=D, a=PARTS)
                        sp.dma_start(op[hg][PR * r:PR * (r + 1), :, :], src).then_inc(s_ld[hg], 16)

            def load_shift(b, hg):
                g = b * HG + hg
                sp.wait_ge(s_mxT, g + 1)
                for a in range(PARTS):
                    n = J * NT
                    sp.dma_start(q_op[hg][SH + a:SH + a + 1, :, :].rearrange("o j (n t) -> o (j n) t", t=P),
                                 mxT[n * a:n * (a + 1), hg % 2, :]).then_inc(s_sh[hg], 16)

            sp.wait_ge(s_const, 3)
            for hg in range(HG - 1):
                load_group(0, hg)
            load_shift(0, 0)

            def feed(b):
                last = isinstance(b, int) and b == B - 1
                for hg in range(HG):
                    if hg == 0:
                        load_group(b, HG - 1)
                    elif not last:
                        load_group(b + 1, hg - 1)
                    if hg < HG - 1:
                        load_shift(b, hg + 1)
                    elif not last:
                        load_shift(b + 1, 0)

            sequences(sp, feed)

            sp.wait_ge(s_tab, N_TAB)
            sp.wait_ge(s_put, B * (16 * NC))
            sp.wait_ge(s_exp, NG * J * NT)
            sp.wait_ge(s_pv, NG * NT)
            for e in range(E):
                at = sp.value_load(pad_row[0:1, e:e + 1], min_val=0, max_val=E * REGION - TR)
                fill(at, e)
            sp.wait_ge(s_fill, 16 * (2 * K2 * E))

            def load_tile(it, u):
                t = it * RING + u
                at = sp.value_load(tab_row[0:1, bass.ds(t, 1)], min_val=0, max_val=E * REGION + (E - 1) * TR)
                wait(sp, s_rid, t - RING + 1)
                wait(sp, s_tT, t - RING + 1)
                sp.dma_start(y_tile[:, u, :, :], slots[bass.ds(at, TR), :].rearrange("(h p) c -> p h c", p=P)).then_inc(s_yl[u], 16)

            for u in range(RING):
                load_tile(0, u)
            with sp.Fori(1, TILES // RING) as it:
                for u in range(RING):
                    load_tile(it, u)

            for par in range(2):
                sp.wait_ge(s_res[par], (TILES // 2) * (16 * TH))
            sp.wait_ge(s_rid, TILES)
            sp.wait_ge(s_tT, TILES)
            by_seq = results[0:K2 * B * S, :].rearrange("(n p k) c -> p n k c", p=P, k=K2)

            def load_results(it, u):
                b = it * RING + u
                wait(sp, s_fin, b - RING + 1)
                sp.dma_start(r_ring[:, u, :, :, :], by_seq[:, bass.ds(b * NT, NT), :, :]).then_inc(s_rl[u], 16)

            for u in range(RING):
                load_results(0, u)
            with sp.Fori(1, B // RING) as it:
                for u in range(RING):
                    load_results(it, u)
            sp.wait_ge(s_out, 16 * B)

        @block.gpsimd
        def _(pool):
            nc.gpsimd.memset(wo_sb[:, :, :], 0.0).then_inc(s_pad, 1)
            nc.gpsimd.memset(zero_sb[:, :, :], 0.0).then_inc(s_pad, 1)
            nc.gpsimd.memset(neg_half[:, :], -0.5).then_inc(s_pad, 1)
            nc.gpsimd.memset(e_const[:, :], 2.718281828459045).then_inc(s_pad, 1)
            nc.gpsimd.memset(v_op[:, :, :, :, :], 0.0).then_inc(s_pad, 1)
            pool.wait_ge(s_pad, 5)
            nc.gpsimd.memset(v_op[:, :, :, :, 0:1], 1.0).then_inc(s_pad, 1)
            pool.wait_ge(s_pad, 6)
            pool.wait_ge(s_ve, 1)
            nc.gpsimd.tensor_tensor(rstd[:, :], var_eps[:, :], neg_half[:, :], ALU.pow).then_inc(s_rstd, 1)
            pool.wait_ge(s_v, B)

            def gather_v(b, hg):
                wait(pool, s_pv, NT * (b * HG + hg - HG + 1))
                src = v_all[:, b, :, J * D * hg:J * D * (hg + 1)].rearrange("p n (j d) -> p n j d", j=J)
                nc.gpsimd.tensor_copy(v_op[:, hg, :, :, 1:1 + D], src).then_inc(s_vop, 1)

            def ln2_rstd(b):
                pool.wait_ge(s_ve, b + 2)
                nc.gpsimd.tensor_tensor(rstd[:, 0:NT], var_eps[:, 0:NT], neg_half[:, 0:NT], ALU.pow).then_inc(s_rstd, 1)

            def put_rows(b):
                pool.wait_ge(s_slot, b + 1)
                pool.sem_inc(s_go, 1)
                for i in range(NT):
                    for k in range(K2):
                        nc.gpsimd.indirect_dma_start(slots, bass.IndirectOffsetOnAxis(slot_u[:, K2 * i + k:K2 * i + k + 1], 0),
                                                     y2[:, i, k, :], None).then_inc(s_put, 16)

            gather_v(0, 0)
            gather_v(0, 1)

            def gather_and_route(b):
                first, last = isinstance(b, int) and b == 0, isinstance(b, int) and b == B - 1
                gather_v(b, 2)
                if not first:
                    ln2_rstd(b - 1)
                gather_v(b, 3)
                if not last:
                    gather_v(b + 1, 0)
                    gather_v(b + 1, 1)
                if not first:
                    put_rows(b - 1)

            sequences(pool, gather_and_route)
            ln2_rstd(B - 1)
            put_rows(B - 1)
            pool.wait_ge(s_gd, B)
            nc.gpsimd.tensor_tensor(l_exp[:, :], e_const[:, :], l_diff[:, :], ALU.pow).then_inc(s_ge, 1)

            def put_results(t, par):
                pool.wait_ge(s_rt2, t + 1)
                pool.sem_inc(s_go, 1)
                for h in range(TH):
                    nc.gpsimd.indirect_dma_start(results, bass.IndirectOffsetOnAxis(row_id[:, par, h:h + 1], 0),
                                                 r_tile[:, par, h, :], None).then_inc(s_res[par], 16)

            with pool.Fori(0, TILES // 2) as it:
                put_results(it * 2, 0)
                put_results(it * 2 + 1, 1)

        @block.scalar
        def _(act):
            act.wait_ge(s_w, 16 * N_W)

            def project(b, par, it):
                act.wait_ge(s_xnTp, b + 1)
                nc.scalar.activation(xnT[:, par, :], ps[:, par, :], ACT.Copy).then_inc(s_xnT, 1)
                for w, (ready, bias) in enumerate(((s_qp, bq_sb), (s_kp, bk_sb))):
                    act.wait_ge(ready, b + 1)
                    wait(act, s_lo, 2 * (b - 1))
                    wait(act, s_scr[par], it * (16 * N_SCR))
                    nc.scalar.activation(qk32[:, par, w, :], ps[:, 2 + 2 * w + par, :], ACT.Identity,
                                         bias=bias[:, 0:1]).then_inc(s_qk32, 1)
                    act.wait_ge(s_qk32, 2 * b + w + 1)
                    nc.scalar.activation(parts[:, par, w, 0, :], qk32[:, par, w, :], ACT.Copy).then_inc(s_hi, 1)
                for w in range(2):
                    act.wait_ge(s_rest, 2 * b + w + 1)
                    nc.scalar.activation(parts[:, par, w, 1, :], rest[:, w, :], ACT.Copy).then_inc(s_mid, 1)

            project(0, 0, 0)
            project(1, 1, 0)
            with act.Fori(1, B // 2) as it:
                project(it * 2, 0, it)
                project(it * 2 + 1, 1, it)

            def copy_yT(b):
                act.wait_ge(s_yTp, b + 1)
                wait(act, s_lgp, b)
                nc.scalar.activation(yT_now[:, :], ps[:, BK_M, :], ACT.Copy)
                nc.scalar.activation(yT[:, b, :], ps[:, BK_M, :], ACT.Copy).then_inc(s_yT, 1)

            def exps(b):
                first = isinstance(b, int) and b == 0
                for hg in range(HG):
                    g = b * HG + hg
                    for i in range(NT):
                        wait(act, s_pv, (g - 1) * NT + i + 1)
                        for j in range(J):
                            n = g * (J * NT) + i * J + j
                            act.wait_ge(s_sb, n + 1)
                            nc.scalar.activation(probs[:, i, j, :], ps[:, BK_S + j % 2, :],
                                                 ACT.Exp, scale=float(D) ** -0.5).then_inc(s_exp, 1)
                            if hg == 2 and i * J + j == YT_STEP + 1 and not first:
                                copy_yT(b - 1)

            sequences(act, exps)

            act.wait_ge(s_wffn, 16 * 8)
            act.wait_ge(s_pv, NG * NT)

            def gelus(b, par):
                for c in range(FC):
                    act.wait_ge(s_up, b * FC + c + 1)
                    if c == 0:
                        wait(act, s_dn, b - 1)
                    nc.scalar.activation(hid[:, par, c, :], ps[:, UP0 + c, :], ACT.Gelu_apprx_tanh,
                                         bias=b1_sb[:, E, c:c + 1]).then_inc(s_gelu, 1)

            gelus(0, 0)
            copy_yT(B - 1)
            gelus(1, 1)
            with act.Fori(1, B // 2) as it:
                gelus(it * 2, 0)
                gelus(it * 2 + 1, 1)

            act.wait_ge(s_dn, B)

            def tile_gelus(t, par):
                act.wait_ge(s_w1c, t + 1)
                for c in range(FC):
                    if c % 2 == 0:
                        act.wait_ge(s_tup, t * (FC // 2) + c // 2 + 1)
                    if c == 0:
                        wait(act, s_tdn, t - 1)
                    nc.scalar.activation(hid_tile[:, par, c, :], ps[:, BK_TU + 2 * par + c // 2, TR * (c % 2):TR * (c % 2 + 1)],
                                         ACT.Gelu_apprx_tanh, bias=b1_cur[:, par, c:c + 1]).then_inc(s_th, 1)

            tile_gelus(0, 0)
            tile_gelus(1, 1)
            with act.Fori(1, TILES // 2) as it:
                tile_gelus(it * 2, 0)
                tile_gelus(it * 2 + 1, 1)

            with act.Fori(0, B) as b:
                act.wait_ge(s_fin, b + 1)
                act.dma_start(out.rearrange("(n p) c -> p n c", p=P)[:, bass.ds(b * NT, NT), :],
                              x_sb[:, bass.ds(b * NT, NT), :]).then_inc(s_out, 16)

        @block.vector
        def _(dve):
            for hg in range(HG):
                nc.vector.memset(q_op[hg][64:P, :, :], 0.0)
                last = nc.vector.memset(k_op[hg][64:P, :, :], 0.0)
            last.then_inc(s_const, 1)
            dve.wait_ge(s_const, 1)
            for hg in range(HG):
                last = nc.vector.memset(k_op[hg][SH:SH + PARTS, :, :], -1.0)
            last.then_inc(s_const, 2)
            nc.vector.memset(mx_parts[:, :], 0.0).then_inc(s_idbf, 1)
            dve.wait_ge(s_w, 16 * N_W)
            nc.vector.tensor_copy(id_bf[:, :], id_sb[:, :]).then_inc(s_idbf, 1)
            dve.wait_ge(s_x, 16)

            def moments(n, steps, at, part):
                even, odd = stats[:, 0:n, 0:3], stats[:, 0:n, 3:6]
                if part == 0:
                    dve.wait_ge(steps, at)
                    nc.vector.tensor_tensor(mean_d[:, 0:n], even[:, :, 1], odd[:, :, 1], ALU.subtract).then_inc(steps, 1)
                    nc.vector.tensor_tensor(mean[:, 0:n], even[:, :, 1], odd[:, :, 1], ALU.add).then_inc(steps, 1)
                    nc.vector.tensor_tensor(dev[:, 0:n], even[:, :, 2], odd[:, :, 2], ALU.add).then_inc(steps, 1)
                elif part == 1:
                    dve.wait_ge(steps, at + 3)
                    nc.vector.tensor_tensor(mean_d2[:, 0:n], mean_d[:, 0:n], mean_d[:, 0:n], ALU.mult).then_inc(steps, 1)
                    nc.vector.tensor_scalar(mean[:, 0:n], mean[:, 0:n], 0.5, None, ALU.mult).then_inc(steps, 1)
                    nc.vector.tensor_scalar(dev[:, 0:n], dev[:, 0:n], 1.0 / C, EPS, ALU.mult, ALU.add).then_inc(steps, 1)
                else:
                    dve.wait_ge(steps, at + 6)
                    nc.vector.scalar_tensor_tensor(out=var_eps[:, 0:n], in0=mean_d2[:, 0:n], scalar=0.25, in1=dev[:, 0:n],
                                                   op0=ALU.mult, op1=ALU.add).then_inc(s_ve, 1)

            with dve.Fori(0, B) as b:
                for i in range(NT):
                    t = e_tile(b, i)
                    last = nc.vector.bn_stats(stats[:, t, :], x_sb[:, t, :])
                last.then_inc(s_st, 1)
            for part in range(3):
                moments(B * NT, s_st, B, part)
            dve.wait_ge(s_rstd, 1)

            def normalise(b, par):
                wait(dve, s_xnTp, b - 1)
                for i in range(NT):
                    t = e_tile(b, i)
                    last = nc.vector.tensor_scalar(xn[:, par, i, :], x_sb[:, t, :], mean[:, bass.ds(t, 1)], rstd[:, bass.ds(t, 1)],
                                                   ALU.subtract, ALU.mult)
                last.then_inc(s_xn, 1)

            def split(b, par):
                dve.wait_ge(s_vp, b + 1)
                nc.vector.tensor_tensor(v_all[:, b, :, :], ps[:, 6 + par, :].rearrange("p (n c) -> p n c", c=C),
                                        bv_sb[:, :].unsqueeze(1).to_broadcast([P, NT, C]), ALU.add).then_inc(s_v, 1)
                for w in range(2):
                    dve.wait_ge(s_hi, 2 * b + w + 1)
                    wait(dve, s_lo, 2 * b + w - 1)
                    nc.vector.tensor_tensor(rest[:, w, :], qk32[:, par, w, :], parts[:, par, w, 0, :],
                                            ALU.subtract).then_inc(s_rest, 1)
                for w in range(2):
                    dve.wait_ge(s_mid, 2 * b + w + 1)
                    nc.vector.tensor_tensor(parts[:, par, w, 2, :], rest[:, w, :], parts[:, par, w, 1, :],
                                            ALU.subtract).then_inc(s_lo, 1)

            normalise(0, 0)
            normalise(1, 1)
            split(0, 0)
            with dve.Fori(1, B // 2) as it:
                normalise(it * 2, 0)
                split(it * 2 - 1, 1)
                normalise(it * 2 + 1, 1)
                split(it * 2, 0)
            split(B - 1, 1)

            PAIRS = J * NT // 2

            def row_max(g, p, slot):
                dve.wait_ge(s_sa, g * PAIRS + p + 1)
                bank = BK_A + 2 * (p % 2)
                nc.vector.reduce_max(mx[:, slot % 2, 2 * p:2 * p + 2], ps[:, bank:bank + 2, :], AX.X).then_inc(s_max, 1)

            def max_split(g, slot, step):
                m = mx[:, slot % 2, :]
                if step == 0:
                    dve.wait_ge(s_max, (g + 1) * PAIRS)
                    wait(dve, s_mxTp, g)
                    nc.vector.tensor_copy(mx_parts[:, 0:J * NT], m).then_inc(s_ms, 1)
                elif step == 1:
                    dve.wait_ge(s_ms, g * 3 + 1)
                    nc.vector.tensor_tensor(mx_rest[:, :], m, mx_parts[:, 0:J * NT], ALU.subtract).then_inc(s_ms, 1)
                elif step == 2:
                    dve.wait_ge(s_ms, g * 3 + 2)
                    nc.vector.tensor_copy(mx_parts[:, J * NT:2 * J * NT], mx_rest[:, :]).then_inc(s_ms, 1)
                else:
                    dve.wait_ge(s_ms, g * 3 + 3)
                    nc.vector.tensor_tensor(mx_parts[:, 2 * J * NT:3 * J * NT], mx_rest[:, :], mx_parts[:, J * NT:2 * J * NT],
                                            ALU.subtract).then_inc(s_msp, 1)

            def max_out(b, hg):
                g = b * HG + hg
                dve.wait_ge(s_mxTp, g + 1)
                if hg >= 2:
                    dve.wait_ge(s_sh[hg - 2], (b + 1) * (16 * PARTS))
                else:
                    wait(dve, s_sh[hg + 2], b * (16 * PARTS))
                nc.vector.tensor_copy(mxT[:, hg % 2, :], ps[0:PARTS * J * NT, BK_M, 0:P // 2].bitcast(bf16)).then_inc(s_mxT, 1)

            def out_norm(b, hg, step):
                g = b * HG + hg
                if step == 0:
                    wait(dve, s_o, g)
                    dve.wait_ge(s_pv, (g + 1) * NT)
                    nc.vector.transpose(o_t[:, :, :].rearrange("p a c -> p (a c)"), ps[:, BK_O, :]).then_inc(s_ot, 1)
                elif step == 1:
                    dve.wait_ge(s_ot, g + 1)
                    nc.vector.reciprocal(o_rec[:, :], o_t[:, :, 0]).then_inc(s_orec, 1)
                elif step == 2:
                    dve.wait_ge(s_orec, g + 1)
                    nc.vector.scalar_tensor_tensor(out=o_t[:, :, 1:1 + D], in0=o_t[:, :, 1:1 + D],
                                                   scalar=mask_sb[:, hg:hg + 1],
                                                   in1=o_rec[:, :].unsqueeze(2).to_broadcast([P, S // 32, D]),
                                                   op0=ALU.mult, op1=ALU.mult).then_inc(s_onrm, 1)
                else:
                    dve.wait_ge(s_onrm, g + 1)
                    if hg == 0:
                        wait(dve, s_ap, b)
                    nc.vector.transpose(o_sb[:, hg, :], o_t[:, :, :].rearrange("p a c -> p (a c)")).then_inc(s_o, 1)

            def residual(b):
                dve.wait_ge(s_ap, b + 1)
                sl = x_sb[:, bass.ds(b * NT, NT), :]
                nc.vector.tensor_tensor(sl, ps[:, BK_M, :].rearrange("p (n c) -> p n c", c=C), sl, ALU.add).then_inc(s_x2, 1)

            def ln2_stats(b):
                dve.wait_ge(s_x2, b + 1)
                dve.sem_inc(s_bn, 1)
                for i in range(NT):
                    last = nc.vector.bn_stats(stats[:, i, :], x_sb[:, e_tile(b, i), :])
                last.then_inc(s_st, 1)

            def ln2_moments(b, part):
                moments(NT, s_st, b * 7 + B + 7, part)

            def ln2_normalise(b, some):
                if 0 in some:
                    dve.wait_ge(s_rstd, b + 2)
                    wait(dve, s_put, b * (16 * NC))
                    wait(dve, s_yTp, b)
                for i in some:
                    last = nc.vector.tensor_scalar(y2[:, i, :, 0:C], x_sb[:, e_tile(b, i), :].unsqueeze(1).to_broadcast([P, K2, C]),
                                                   mean[:, i:i + 1], rstd[:, i:i + 1], ALU.subtract, ALU.mult)
                if NT - 1 in some:
                    last.then_inc(s_yn, 1)
                    nc.vector.tensor_copy(y2[:, :, :, C].bitcast(u32), ids_sb[:, bass.ds(b * NT, NT), :]).then_inc(s_y, 1)

            def router_step(b, step):
                if step == 0:
                    dve.wait_ge(s_lgp, b + 1)
                    nc.vector.tensor_copy(logits[:, :, :], ps[:, BK_M, 0:NT * E].rearrange("p (n e) -> p n e", e=E)).then_inc(s_rt, 1)
                elif step == 1:
                    dve.wait_ge(s_rt, b * R + 1)
                    nc.vector.reduce_max(top1[:, :], logits[:, :, :], AX.X)
                    for i in range(NT):
                        last = nc.vector.max(top8[:, i, :], logits[:, i, :])
                    last.then_inc(s_rt, 1)
                elif step == 2:
                    dve.wait_ge(s_rt, b * R + 2)
                    nc.vector.tensor_tensor(l_diff[:, bass.ds(b * NT, NT)], top8[:, :, 1], top1[:, :], ALU.subtract).then_inc(s_gd, 1)
                    for i in range(NT):
                        last = nc.vector.max_index(top_i[:, i, :], top8[:, i, :], logits[:, i, :])
                    last.then_inc(s_rt, 1)
                elif step == 3:
                    dve.wait_ge(s_rt, b * R + 3)
                    nc.vector.tensor_copy(top_if[:, :, :], top_i[:, :, 0:K2]).then_inc(s_rt, 1)
                else:
                    dve.wait_ge(s_rt, b * R + 4)
                    wait(dve, s_rk, b)
                    nc.vector.tensor_tensor(chosen[:, :, :], iota_sb[:, :].unsqueeze(1).to_broadcast([P, NC, E]),
                                            top_if[:, :, :].rearrange("p n k -> p (n k)").unsqueeze(2).to_broadcast([P, NC, E]),
                                            ALU.is_equal).then_inc(s_rt, 1)

            def slot_step(b, step):
                if step == 0:
                    dve.wait_ge(s_rk, b + 1)
                    nc.vector.tensor_tensor(at_f[:, :, :], ps[:, BK_M, 0:NC * E].rearrange("p (c e) -> p c e", e=E),
                                            chosen[:, :, :], ALU.mult).then_inc(s_sl, 1)
                elif step == 1:
                    dve.wait_ge(s_sl, b * 2 + 1)
                    nc.vector.reduce_sum(slot_f[:, :], at_f[:, :, :], AX.X).then_inc(s_sl, 1)
                else:
                    dve.wait_ge(s_sl, b * 2 + 2)
                    nc.vector.tensor_copy(slot_u[:, :], slot_f[:, :]).then_inc(s_slot, 1)

            def count_step(b, step):
                if step == 0:
                    dve.wait_ge(s_rt, (b + 1) * R)
                    nc.vector.reduce_sum(seq_n[:, :], chosen[:, :, :].rearrange("p c e -> p e c"), AX.X).then_inc(s_cn, 1)
                elif step == 1:
                    dve.wait_ge(s_cn, (b + 1) * Q + 1)
                    nc.vector.tensor_tensor(run_n[:, :], run_n[:, :], seq_n[:, :], ALU.add).then_inc(s_cn, 1)
                else:
                    dve.wait_ge(s_cn, (b + 1) * Q + 2)
                    dve.wait_ge(s_sl, b * 2 + 1)
                    nc.vector.tensor_copy(run_bf[:, :], run_n[:, :]).then_inc(s_cn, 1)

            with dve.Fori(0, B) as b:
                sl = x_sb[:, bass.ds(b * NT, NT), :]
                nc.vector.tensor_tensor(sl, sl, bo_sb[:, :].unsqueeze(1).to_broadcast([P, NT, C]), ALU.add).then_inc(s_xbo, 1)
            dve.wait_ge(s_xbo, B)

            dve.wait_ge(s_route, 16 * N_ROUTE)
            nc.vector.tensor_copy(tri_bf[:, :], tri_f[:, :]).then_inc(s_tab, 1)
            nc.vector.tensor_copy(reg_bf[:, :], reg_f[:, :]).then_inc(s_tab, 1)
            nc.vector.memset(ones_bf[:, :], 1.0).then_inc(s_tab, 1)
            nc.vector.memset(run_n[:, :], 0.0).then_inc(s_tab, 1)
            nc.vector.memset(run_bf[:, :], 0.0).then_inc(s_cn, Q)
            dve.wait_ge(s_tab, N_MAT)
            dve.wait_ge(s_cn, Q)

            for p in range(PAIRS):
                row_max(0, p, 0)
            for p in range(PAIRS):
                row_max(1, p, 1)
                if p == 0:
                    for step in range(4):
                        max_split(0, 0, step)
                if p == 4:
                    max_out(0, 0)

            def attend(b):
                first, last = isinstance(b, int) and b == 0, isinstance(b, int) and b == B - 1
                for hg in range(HG):
                    g = b * HG + hg
                    ahead = not last or hg < HG - 2
                    nxt = not last or hg < HG - 1
                    for p in range(PAIRS):
                        if ahead:
                            row_max(g + 2, p, hg)
                        if nxt and p < 4:
                            max_split(g + 1, hg + 1, p)
                        if nxt and p == (5 if hg == 1 else 4):
                            if hg < HG - 1:
                                max_out(b, hg + 1)
                            else:
                                max_out(b + 1, 0)
                        if 3 <= p < 7 and hg > 0:
                            out_norm(b, hg - 1, p - 3)
                        elif 3 <= p < 7 and not first:
                            out_norm(b - 1, HG - 1, p - 3)
                        if not first:
                            if hg == 1:
                                if p == 3:
                                    residual(b - 1)
                                if p == 5:
                                    ln2_stats(b - 1)
                                if p >= 6:
                                    ln2_moments(b - 1, p - 6)
                            if hg == 2:
                                if p == 0:
                                    ln2_moments(b - 1, 2)
                                if p == 2 or p == 3:
                                    ln2_normalise(b - 1, (2 * p - 4, 2 * p - 3))
                            if hg == 3:
                                if p < 5:
                                    router_step(b - 1, p)
                                if p >= 5:
                                    count_step(b - 1, p - 5)
                                if p >= 6:
                                    slot_step(b - 1, p - 6)
                                if p == 7:
                                    slot_step(b - 1, 2)
            sequences(dve, attend)
            for step in range(4):
                out_norm(B - 1, HG - 1, step)
            residual(B - 1)

            ln2_stats(B - 1)
            for part in range(3):
                ln2_moments(B - 1, part)
            ln2_normalise(B - 1, range(NT))
            for step in range(5):
                router_step(B - 1, step)

            def add_shared(b, par):
                dve.wait_ge(s_dn, b + 1)
                sl = x_sb[:, bass.ds(b * NT, NT), :]
                nc.vector.tensor_tensor(sl, ps[:, DN0 + par, :].rearrange("p (n c) -> p n c", c=C), sl, ALU.add).then_inc(s_mix, 1)

            add_shared(0, 0)
            add_shared(1, 1)
            for step in range(3):
                slot_step(B - 1, step)
            for step in range(3):
                count_step(B - 1, step)
            add_shared(2, 0)

            def step(n, instruction):
                instruction.then_inc(s_tab, 1)
                dve.wait_ge(s_tab, N_MAT + n)

            n_thr = B * S // TR
            dve.wait_ge(s_cntp, 1)
            step(1, nc.vector.tensor_copy(cnt[:, :], ps[0:1, BK_M, 0:E]))
            step(2, nc.vector.tensor_tensor(over[:, :, :], cnt[:, :].unsqueeze(2).to_broadcast([1, E, n_thr]),
                                            thr_sb[:, :].unsqueeze(1).to_broadcast([1, E, n_thr]), ALU.is_gt))
            step(3, nc.vector.reduce_sum(n_tiles[:, :], over[:, :, :], AX.X))
            step(4, nc.vector.tensor_tensor(upto[:, :, :], n_tiles[:, :].unsqueeze(1).to_broadcast([1, E, E]), tri8_sb[:, :, :], ALU.mult))
            step(5, nc.vector.reduce_sum(tile_end[:, :], upto[:, :, :], AX.X))
            step(6, nc.vector.tensor_tensor(past[:, :, :], tid_sb[:, :].unsqueeze(2).to_broadcast([1, TILES, E]),
                                            tile_end[:, :].unsqueeze(1).to_broadcast([1, TILES, E]), ALU.is_ge))
            step(7, nc.vector.reduce_sum(t_exp[:, :], past[:, :, :], AX.X))
            step(8, nc.vector.tensor_tensor(past_n[:, :, :], past[:, :, :], n_tiles[:, :].unsqueeze(1).to_broadcast([1, TILES, E]), ALU.mult))
            step(9, nc.vector.reduce_sum(t_first[:, :], past_n[:, :, :], AX.X))
            step(10, nc.vector.tensor_tensor(t_row[:, :], tid_sb[:, :], t_first[:, :], ALU.subtract))
            step(11, nc.vector.tensor_scalar(t_row[:, :], t_row[:, :], float(TR), None, ALU.mult))
            step(12, nc.vector.scalar_tensor_tensor(out=t_row[:, :], in0=t_exp[:, :], scalar=float(REGION), in1=t_row[:, :],
                                                    op0=ALU.mult, op1=ALU.add))
            step(13, nc.vector.tensor_copy(tab_row[:, :], t_row[:, :]))
            step(14, nc.vector.tensor_scalar(tab_e[:, :], t_exp[:, :], float(E - 1), None, ALU.min))
            step(15, nc.vector.tensor_tensor(pad_f[:, :], cnt[:, :], regr_sb[:, :], ALU.add))
            step(16, nc.vector.tensor_copy(pad_row[:, :], pad_f[:, :]))

            add_shared(3, 1)
            with dve.Fori(2, B // 2) as it:
                add_shared(it * 2, 0)
                add_shared(it * 2 + 1, 1)

            def expert_of(t):
                return dve.value_load(tab_e[0:1, bass.ds(t, 1)], min_val=0, max_val=E - 1)

            def copy_w1(t, par):
                e = expert_of(t)
                nc.vector.tensor_copy(w1_cur[:, par, :], w1_sb[:, e, :])
                nc.vector.tensor_copy(b1_cur[:, par, :], b1_sb[:, e, :]).then_inc(s_w1c, 1)

            def copy_w2(t, par):
                e = expert_of(t)
                nc.vector.tensor_copy(w2_cur[:, par, :, :], w2_sb[:, e, :, :]).then_inc(s_w2c, 1)

            def tile_yT(t, par):
                dve.wait_ge(s_tT, t + 1)
                wait(dve, s_tup, (t - 1) * (FC // 2))
                wait(dve, s_th, (t - 1) * FC)
                nc.vector.tensor_copy(yT_tile[:, par, :], ps[:, BK_TT + par, 0:TR]).then_inc(s_tyT, 1)

            def tile_result(t, par, before, u):
                wait(dve, s_res[par], before * (16 * TH))
                nc.vector.tensor_copy(row_id[:, par, :], y_tile[:, u, :, C].bitcast(u32)).then_inc(s_rid, 1)
                e = expert_of(t)
                dve.wait_ge(s_tdn, t + 1)
                nc.vector.tensor_tensor(r_tile[:, par, :, :], ps[:, BK_TD + par, 0:TH * C].rearrange("p (h c) -> p h c", c=C),
                                        b2_sb[:, bass.ds(e, 1), :].to_broadcast([P, TH, C]), ALU.add).then_inc(s_rt2, 1)

            def tile_step(it, u):
                t = it * RING + u
                peeled = isinstance(t, int)
                if not (peeled and t == 0):
                    prev = t - 1
                    if peeled:
                        before = prev // 2
                    else:
                        before = it * (RING // 2) + (u - 1) // 2
                    tile_result(prev, (u - 1) % 2, before, (u - 1) % RING)
                if not (peeled and t + 1 >= TILES):
                    copy_w2(t + 1, (u + 1) % 2)
                if not (peeled and t + 2 >= TILES):
                    tile_yT(t + 2, u % 2)
                    copy_w1(t + 2, u % 2)

            copy_w1(0, 0)
            copy_w1(1, 1)
            copy_w2(0, 0)
            tile_yT(0, 0)
            tile_yT(1, 1)
            for u in range(RING):
                tile_step(0, u)
            with dve.Fori(1, TILES // RING - 1) as it:
                for u in range(RING):
                    tile_step(it, u)
            for u in range(RING):
                tile_step(TILES // RING - 1, u)
            tile_result(TILES - 1, 1, (TILES - 1) // 2, RING - 1)

            dve.wait_ge(s_ge, 1)
            nc.vector.tensor_scalar(l_sum[:, :], l_exp[:, :], 1.0, None, ALU.add).then_inc(s_gate, 1)
            dve.wait_ge(s_gate, 1)
            nc.vector.reciprocal(top_p[:, 0, :], l_sum[:, :]).then_inc(s_gate, 1)
            dve.wait_ge(s_gate, 2)
            nc.vector.tensor_tensor(top_p[:, 1, :], l_exp[:, :], top_p[:, 0, :], ALU.mult).then_inc(s_gate, 1)
            dve.wait_ge(s_gate, 3)
            dve.wait_ge(s_mix, B)
            nc.vector.tensor_tensor(x_sb[:, :, :], x_sb[:, :, :], b2_sb[:, E:E + 1, :].to_broadcast([P, B * NT, C]), ALU.add).then_inc(s_b2s, 1)
            dve.wait_ge(s_b2s, 1)

            with dve.Fori(0, B // RING) as it:
                for u in range(RING):
                    b = it * RING + u
                    dve.wait_ge(s_rl[u], (it + 1) * 16)
                    for k in range(K2):
                        if k:
                            dve.wait_ge(s_part, b + 1)
                        for i in range(NT):
                            t = e_tile(b, i)
                            last = nc.vector.scalar_tensor_tensor(
                                out=x_sb[:, t, :], in0=r_ring[:, u, i, k, :], scalar=top_p[:, k, bass.ds(t, 1)],
                                in1=x_sb[:, t, :], op0=ALU.mult, op1=ALU.add)
                        last.then_inc(s_fin if k else s_part, 1)

        @block.tensor
        def _(pe):
            pe.wait_ge(s_w, 16 * N_W)
            pe.wait_ge(s_idbf, 2)

            def project(b, par):
                pe.wait_ge(s_xn, b + 1)
                wait(pe, s_xnT, b - 1)
                for i in range(NT):
                    last = nc.tensor.transpose(ps[:, par, P * i:P * (i + 1)], xn[:, par, i, :], id_sb[:, :])
                last.then_inc(s_xnTp, 1)
                pe.wait_ge(s_xnT, b + 1)
                wait(pe, s_qk32, 2 * (b - 1))
                nc.tensor.matmul(ps[:, 2 + par, :], wq_sb[:, :], xnT[:, par, :], start=True, stop=True).then_inc(s_qp, 1)
                nc.tensor.matmul(ps[:, 4 + par, :], wk_sb[:, :], xnT[:, par, :], start=True, stop=True).then_inc(s_kp, 1)
                wait(pe, s_v, b - 1)
                for i in range(NT):
                    last = nc.tensor.matmul(ps[:, 6 + par, C * i:C * (i + 1)], xnT[:, par, P * i:P * (i + 1)], wv_sb[:, :],
                                            start=True, stop=True)
                last.then_inc(s_vp, 1)

            project(0, 0)
            project(1, 1)
            with pe.Fori(1, B // 2) as it:
                project(it * 2, 0)
                project(it * 2 + 1, 1)

            pe.wait_ge(s_xnT, B)
            pe.wait_ge(s_qk32, 2 * B)
            pe.wait_ge(s_v, B)

            def row_scores(b, hg, a):
                j, i = a // NT, a % NT
                if a == 0:
                    pe.wait_ge(s_ld[hg], (b + 1) * (16 * N_LD))
                if a % 2 == 0:
                    wait(pe, s_max, (b * HG + hg) * (J * NT // 2) + a // 2 - 1)
                last = nc.tensor.matmul(ps[:, BK_A + a % 4, :], q_op[hg][0:SH, j, P * i:P * (i + 1)], k_op[hg][0:SH, j, :],
                                        start=True, stop=True)
                if a % 2:
                    last.then_inc(s_sa, 1)

            def key_scores(b, hg, i, j):
                n = (b * HG + hg) * (J * NT) + i * J + j
                if i == 0 and j == 0:
                    pe.wait_ge(s_sh[hg], (b + 1) * (16 * PARTS))
                wait(pe, s_exp, n - 1)
                nc.tensor.matmul(ps[:, BK_S + j % 2, :], k_op[hg][:, j, P * i:P * (i + 1)], q_op[hg][:, j, :],
                                 start=True, stop=True).then_inc(s_sb, 1)

            def pv(b, hg, i):
                g = b * HG + hg
                pe.wait_ge(s_exp, g * (J * NT) + (i + 1) * J)
                if i == 0:
                    wait(pe, s_ot, g)
                    pe.wait_ge(s_vop, g + 1)
                for j in range(J):
                    last = nc.tensor.matmul(ps[32 * j:32 * j + 32, BK_O, :], v_op[:, hg, i, j, :], probs[:, i, j, :],
                                            start=(i == 0), stop=(i == NT - 1))
                last.then_inc(s_pv, 1)

            def max_rows(b, hg):
                g = b * HG + hg
                pe.wait_ge(s_msp, g + 1)
                wait(pe, s_mxT, g)
                if hg == 2:
                    wait(pe, s_x2, b)
                if hg == 0 and not (isinstance(b, int) and b < 2):
                    pe.wait_ge(s_rt, (b - 2) * R + 1)
                if hg == 1 and not (isinstance(b, int) and b < 1):
                    pe.wait_ge(s_cn, b * Q)
                nc.tensor.transpose(ps[:, BK_M, 0:P // 2].bitcast(bf16), mx_parts[:, :], id_bf[:, :]).then_inc(s_mxTp, 1)

            def project_out(b, i):
                if i == 0:
                    pe.wait_ge(s_o, HG * (b + 1))
                    last_b = isinstance(b, int) and b == B - 1
                    pe.wait_ge(s_mxT, NG if last_b else (b + 1) * HG + 2)
                    if last_b:
                        pe.wait_ge(s_cn, (b + 1) * Q)
                for hg in range(HG):
                    last = nc.tensor.matmul(ps[:, BK_M, C * i:C * (i + 1)], o_sb[:, hg, P * i:P * (i + 1)], wo_sb[:, hg, :],
                                            start=(hg == 0), stop=(hg == HG - 1))
                if i == NT - 1:
                    last.then_inc(s_ap, 1)

            def transpose_y(b):
                pe.wait_ge(s_yn, b + 1)
                last_b = isinstance(b, int) and b == B - 1
                if last_b:
                    pe.wait_ge(s_x2, B)
                else:
                    pe.wait_ge(s_mxT, (b + 2) * HG)
                for i in range(NT):
                    last = nc.tensor.transpose(ps[:, BK_M, P * i:P * (i + 1)], y2[:, i, 0, 0:C], id_sb[:, :])
                last.then_inc(s_yTp, 1)

            def router(b):
                pe.wait_ge(s_yT, b + 1)
                for i in range(NT):
                    last = nc.tensor.matmul(ps[:, BK_M, E * i:E * (i + 1)], yT_now[:, P * i:P * (i + 1)], wr_sb[:, :],
                                            start=True, stop=True)
                last.then_inc(s_lgp, 1)

            def ranks(b):
                pe.wait_ge(s_rt, (b + 1) * R)
                pe.wait_ge(s_cn, (b + 1) * Q)
                last_mx = NG if isinstance(b, int) and b >= B - 2 else (b + 2) * HG + 1
                pe.wait_ge(s_mxT, last_mx)
                n = NC * E
                nc.tensor.matmul(ps[:, BK_M, 0:n], tri_bf[:, :], chosen[:, :, :].rearrange("p c e -> p (c e)"),
                                 start=True, stop=False)
                for d in range(1, NC):
                    nc.tensor.matmul(ps[:, BK_M, E * d:n], ones_bf[:, :],
                                     chosen[:, 0:NC - d, :].rearrange("p c e -> p (c e)"), start=False, stop=False)
                every = ps[:, BK_M, 0:n].rearrange("p (c e) -> p c e", e=E)
                nc.tensor.matmul(every, ones_bf[:, :], run_bf[:, :].unsqueeze(1).to_broadcast([P, NC, E]), start=False, stop=False)
                nc.tensor.matmul(every, ones_bf[:, :], reg_bf[:, :].unsqueeze(1).to_broadcast([P, NC, E]),
                                 start=False, stop=True).then_inc(s_rk, 1)

            for hg in range(2):
                for a in range(J * NT):
                    row_scores(0, hg, a)
                    if hg == 1 and a == 7:
                        max_rows(0, 0)
            pe.wait_ge(s_tab, N_MAT)
            pe.wait_ge(s_wffn, 16 * 8)

            def attend(b):
                first, last_b = isinstance(b, int) and b == 0, isinstance(b, int) and b == B - 1
                for hg in range(HG):
                    for s in range(J * NT):
                        key_scores(b, hg, s // J, s % J)
                        if hg < HG - 2:
                            row_scores(b, hg + 2, s)
                        elif not last_b:
                            row_scores(b + 1, hg - 2, s)
                        if s % J == PV_LAG % J:
                            i = (s - PV_LAG) // J
                            if i >= 0:
                                pv(b, hg, i)
                            elif hg > 0:
                                pv(b, hg - 1, NT + i)
                            elif not first:
                                pv(b - 1, HG - 1, NT + i)
                        if s == (10 if hg == 1 else 8):
                            if hg < HG - 1:
                                max_rows(b, hg + 1)
                            elif not last_b:
                                max_rows(b + 1, 0)
                        if not first:
                            if hg == 1 and s in (1, 2, 4, 5):
                                project_out(b - 1, (1, 2, 4, 5).index(s))
                            if hg == 2 and s == YT_STEP:
                                transpose_y(b - 1)
                            if hg == 2 and s == 15:
                                router(b - 1)
                            if hg == 3 and s == 12:
                                ranks(b - 1)

            sequences(pe, attend)
            for i in range((J * NT - PV_LAG + J - 1) // J, NT):
                pv(B - 1, HG - 1, i)
            for i in range(NT):
                project_out(B - 1, i)

            pe.wait_ge(s_exp, NG * J * NT)
            pe.wait_ge(s_max, NG * J * NT // 2)

            def up(b, par):
                for c in range(FC):
                    wait(pe, s_gelu, (b - 1) * FC + c + 1)
                    nc.tensor.matmul(ps[:, UP0 + c, :], w1_sb[:, E, P * c:P * (c + 1)], yT[:, b, :],
                                     start=True, stop=True).then_inc(s_up, 1)

            def down(b, par):
                pe.wait_ge(s_gelu, (b + 1) * FC)
                wait(pe, s_mix, b - 1)
                for i in range(NT):
                    for c in range(FC):
                        last = nc.tensor.matmul(ps[:, DN0 + par, C * i:C * (i + 1)], hid[:, par, c, P * i:P * (i + 1)],
                                                w2_sb[:, E, c, :], start=(c == 0), stop=(c == FC - 1))
                last.then_inc(s_dn, 1)

            up(0, 0)
            transpose_y(B - 1)
            up(1, 1)
            down(0, 0)
            router(B - 1)
            up(2, 0)
            down(1, 1)
            ranks(B - 1)
            up(3, 1)
            pe.wait_ge(s_cn, (B + 1) * Q)
            nc.tensor.matmul(ps[:, BK_M, 0:E], ones_bf[:, :], run_bf[:, :], start=True, stop=True).then_inc(s_cntp, 1)
            down(2, 0)
            with pe.Fori(2, B // 2) as it:
                up(it * 2, 0)
                down(it * 2 - 1, 1)
                up(it * 2 + 1, 1)
                down(it * 2, 0)
            down(B - 1, 1)

            pe.wait_ge(s_gelu, B * FC)
            pe.wait_ge(s_mix, B)
            pe.wait_ge(s_tab, N_MAT + 1)

            def tile_T(it, u):
                t = it * RING + u
                par = u % 2
                pe.wait_ge(s_yl[u % RING], (it + u // RING + 1) * 16)
                wait(pe, s_tyT, t - 1)
                for h in range(TH):
                    last = nc.tensor.transpose(ps[:, BK_TT + par, P * h:P * (h + 1)], y_tile[:, u % RING, h, 0:C], id_sb[:, :])
                last.then_inc(s_tT, 1)

            def tile_up(t, par):
                pe.wait_ge(s_tyT, t + 1)
                pe.wait_ge(s_w1c, t + 1)
                for c in range(FC):
                    if c % 2 == 0:
                        wait(pe, s_th, (t - 2) * FC + c + 2)
                    last = nc.tensor.matmul(ps[:, BK_TU + 2 * par + c // 2, TR * (c % 2):TR * (c % 2 + 1)],
                                            w1_cur[:, par, P * c:P * (c + 1)], yT_tile[:, par, :], start=True, stop=True)
                    if c % 2:
                        last.then_inc(s_tup, 1)

            def tile_down(t, par):
                pe.wait_ge(s_w2c, t + 1)
                pe.wait_ge(s_th, (t + 1) * FC)
                wait(pe, s_rt2, t - 1)
                for h in range(TH):
                    for c in range(FC):
                        last = nc.tensor.matmul(ps[:, BK_TD + par, C * h:C * (h + 1)], hid_tile[:, par, c, P * h:P * (h + 1)],
                                                w2_cur[:, par, c, :], start=(c == 0), stop=(c == FC - 1))
                last.then_inc(s_tdn, 1)

            def tile_step(it, u):
                t = it * RING + u
                left = TILES - t if isinstance(t, int) else TILES
                if left > 1:
                    tile_up(t + 1, (u + 1) % 2)
                if left > 2:
                    tile_T(it, u + 2)
                tile_down(t, u % 2)

            tile_T(0, 0)
            tile_T(0, 1)
            tile_up(0, 0)
            for u in range(RING):
                tile_step(0, u)
            with pe.Fori(1, TILES // RING - 1) as it:
                for u in range(RING):
                    tile_step(it, u)
            for u in range(RING):
                tile_step(TILES // RING - 1, u)


def kernel(**a):
    import numpy as np
    import concourse.bacc as bacc
    from concourse import mybir as mb
    from concourse.bass_utils import run_bass_kernel_spmd as run

    a = {k.replace("L0_attn_", "a_").replace("L0_ffn_", "f_"): np.asarray(v) for k, v in a.items()}
    with_shared = lambda routed, shared: np.concatenate([routed, shared[None]], axis=0)
    ins = {
        "x": a["a_x"].reshape(B * S, C),
        "WqT": a["a_Wq"].T, "WkT": a["a_Wk"].T, "WvT": a["a_Wv"].T, "WoT": a["a_Wo"].T,
        "bq": a["a_bq"], "bk": a["a_bk"], "bv": a["a_bv"], "bo": a["a_bo"], "head_mask": a["a_head_mask"],
        "W1": with_shared(a["f_Wfc"], a["f_Wfc_s"]).transpose(1, 0, 2),
        "b1": with_shared(a["f_bfc"], a["f_bfc_s"]).reshape(NE, FC, P).transpose(2, 0, 1),
        "W2": with_shared(a["f_Wproj"], a["f_Wproj_s"]).reshape(NE, FC, P, C).transpose(2, 0, 1, 3),
        "b2": with_shared(a["f_bproj"], a["f_bproj_s"]),
        "Wr": a["f_Wr"],
        "ident": np.eye(P, dtype=np.float32),
        "tri": np.triu(np.ones((P, P), np.float32), 1),
        "region_at": np.concatenate([np.arange(E, dtype=np.float32)[None] * REGION, np.zeros((P - 1, E), np.float32)]),
        "region_row": np.arange(E, dtype=np.float32)[None] * REGION,
        "row_ids": np.arange(K2 * B * S, dtype=np.uint32).reshape(B * S, K2),
        "dump_ids": (K2 * B * S + np.arange(K2 * E * TR, dtype=np.uint32)).reshape(K2 * E, TH, P, 1).transpose(2, 0, 1, 3),
        "thresholds": np.arange(0, B * S, TR, dtype=np.float32)[None],
        "tri8": np.tril(np.ones((E, E), np.float32))[None],
        "tile_ids": np.arange(TILES, dtype=np.float32)[None],
        "iota8": np.tile(np.arange(E, dtype=np.float32), (P, 1)),
    }
    nc = bacc.Bacc("TRN2", target_bir_lowering=False, num_devices=1)
    arrays, aps = {}, {}
    for name, v in ins.items():
        v = np.ascontiguousarray(v)
        arrays[f"in_{name}"] = v
        aps[name] = nc.dram_tensor(f"in_{name}", v.shape, mb.dt.from_np(v.dtype), kind="ExternalInput").ap()
    aps["out"] = nc.dram_tensor("out_0", (B * S, C), mb.dt.float32, kind="ExternalOutput").ap()
    block_kernel(nc, **aps)
    r = run(nc, [arrays], core_ids=[0])
    return r.results[0]["out_0"].reshape(B, S, C)
```

```python
import struct

import concourse.bass as bass
from concourse import mybir
from contextlib import ExitStack

B, S, C = 8, 512, 128
H, D = 16, 8
J = 4
HG = H // J
P = 128
NT = S // P
PARTS = 3
PR = PARTS * D
KR = PARTS * PR
SHIFTS = 2
SH = 96
E, F = 8, 512
NE = E + 1
FC = F // P
EPS = 1e-5
TWO_MINUS_ONES = struct.unpack("f", struct.pack("I", 0xBF80BF80))[0]
NG = B * HG
K2 = 2
NC = NT * K2
TR = 128
TH = TR // P
TILES = K2 * B * S // TR + E - 1
REGION = B * S + TR
ROW = C + 1
DEEP = 4
EARLY = 4
RING = 8
TABLE = -(-TILES // RING) * RING
AHEAD = 5
BY_POOL = (2, 3)
TQ = 4


def block_kernel(nc, x, WqT, WkT, WvT, WoT, bq, bk, bv, bo, head_mask, W1, b1, W2, b2, Wr, ident, iota8,
                 tri, region_at, row_ids, dump_ids, thresholds, tri8, tile_ids, tile_slots, region_row, out):
    f32, bf16, u32 = mybir.dt.float32, mybir.dt.bfloat16, mybir.dt.uint32
    ALU, ACT, AX = mybir.AluOpType, mybir.ActivationFunctionType, mybir.AxisListType

    q_scr = nc.dram_tensor("q_scr", (B, H * D, PARTS * S), bf16, kind="Internal").ap()
    k_scr = [nc.dram_tensor(f"k_scr{r}", (B, H * D, PARTS * S), bf16, kind="Internal").ap() for r in range(PARTS)]
    slots = nc.dram_tensor("slots", (E * REGION + E * TR, ROW), f32, kind="Internal").ap()
    results = nc.dram_tensor("results", (K2 * B * S + K2 * E * TR, C), f32, kind="Internal").ap()

    ctx = ExitStack()
    with ctx:
        def sb(name, shape, dt=f32):
            return ctx.enter_context(nc.sbuf_tensor(name, shape, dt))

        def sem(name):
            return ctx.enter_context(nc.semaphore(name))

        wq_sb, wk_sb, wv_sb = sb("wq_sb", [P, C]), sb("wk_sb", [P, C]), sb("wv_sb", [P, C])
        wo_sb = sb("wo_sb", [P, C])
        bq_sb, bk_sb = sb("bq_sb", [P, 1]), sb("bk_sb", [P, 1])
        bv_sb, bo_sb = sb("bv_sb", [P, C]), sb("bo_sb", [P, C])
        mask_sb = sb("mask_sb", [P, HG])
        w1_sb, b1_sb = sb("w1_sb", [P, NE, F]), sb("b1_sb", [P, NE, FC])
        w2_sb = sb("w2_sb", [P, NE, FC, C])
        b2_sb = sb("b2_sb", [P, NE, C])
        wr_sb = sb("wr_sb", [P, E])
        id_sb, id_bf = sb("id_sb", [P, P]), sb("id_bf", [P, P], bf16)
        iota_sb = sb("iota_sb", [P, E])
        neg_half, e_const = sb("neg_half", [P, B * NT]), sb("e_const", [P, B * NT])
        x_sb = sb("x_sb", [P, B * NT, C])
        stats = sb("stats", [P, B * NT, 6])
        mean, mean_d = sb("mean", [P, B * NT]), sb("mean_d", [P, B * NT])
        dev, mean_d2 = sb("dev", [P, B * NT]), sb("mean_d2", [P, B * NT])
        quarter, mean_d2q = sb("quarter", [P, NT]), sb("mean_d2q", [P, NT])
        neg_mean, neg_shift = sb("neg_mean", [P, NT]), sb("neg_shift", [P, NT])
        var_eps, rstd = sb("var_eps", [P, B * NT]), sb("rstd", [P, B * NT])
        xn = sb("xn", [P, 2, NT, C])
        xnT = sb("xnT", [P, 2, S])
        qk32 = sb("qk32", [P, 2, 2, S])
        rest = sb("rest", [P, 2, 2, S])
        route_sb = sb("route_sb", [P, NT * K2 * ROW + E * B * S // TR + E * E + K2 * TABLE * E])
        v_all = sb("v_all", [P, B, NT, C])
        q_op = [sb(f"q_op{g}", [P, J, S], bf16) for g in range(HG)]
        k_op = [sb(f"k_op{g}", [P, J, S], bf16) for g in range(HG)]
        v_op = sb("v_op", [P, HG, NT, J, 32])
        mx = sb("mx", [P, 2, J * NT])
        mx_parts = sb("mx_parts", [P, P], bf16)
        mxT = sb("mxT", [SHIFTS * J * NT, 2, P], bf16)
        probs = sb("probs", [P, NT, J, S])
        o_t = sb("o_t", [P, S // 32, 32])
        o_rec = sb("o_rec", [P, S // 32])
        o_all = sb("o_all", [P, S // 32, HG, D])
        o_sb = sb("o_sb", [P, S])
        logits, top8 = sb("logits", [P, NT, E]), sb("top8", [P, NT, 8])
        top_i = sb("top_i", [P, NT, 8], u32)
        l_diff, l_exp = sb("l_diff", [P, B * NT]), sb("l_exp", [P, B * NT])
        l_sum, top_p = sb("l_sum", [P, B * NT]), sb("top_p", [P, K2, B * NT])
        ids_sb = sb("ids_sb", [P, B * NT, K2], u32)
        zero_sb = sb("zero_sb", [P, TH, C])
        dump_sb = sb("dump_sb", [P, K2 * E, TH, 1], u32)
        fill_sb = sb("fill_sb", [P, E, TH, ROW])
        tri_f, tri_bf, ones_bf = sb("tri_f", [P, P]), sb("tri_bf", [P, P], bf16), sb("ones_bf", [P, P], bf16)
        reg_f, reg_bf = sb("reg_f", [P, E]), sb("reg_bf", [P, E], bf16)
        chosen = sb("chosen", [P, NC, E], bf16)
        seq_n = sb("seq_n", [P, E])
        run_bf = sb("run_bf", [P, E], bf16)
        at_f = sb("at_f", [P, NC, E])
        slot_u = sb("slot_u", [P, NC], u32)
        thr_sb, tri8_sb, tid_sb, regr_sb = sb("thr_sb", [1, B * S // TR]), sb("tri8_sb", [1, E, E]), sb("tid_sb", [1, TABLE]), sb("regr_sb", [1, E])
        cnt, n_tiles = sb("cnt", [1, E]), sb("n_tiles", [1, E])
        tile_end = sb("tile_end", [1, E])
        t_exp, t_first, t_row = sb("t_exp", [1, TABLE]), sb("t_first", [1, TABLE]), sb("t_row", [1, TABLE])
        tslot_sb = sb("tslot_sb", [1, TABLE])
        tab_e, tab_row, pad_row = sb("tab_e", [1, TABLE + AHEAD], u32), sb("tab_row", [1, TABLE], u32), sb("pad_row", [1, E], u32)
        b1_cur = sb("b1_cur", [P, TQ, FC])
        row_id = sb("row_id", [P, TQ, TH], u32)
        yT = v_all.rearrange("p b n c -> p b (n c)")
        yT_now = xnT[:, 0, :]
        parts = probs.rearrange("p i j s -> p (i j s)").bitcast(bf16)[:, 0:DEEP * 2 * PARTS * S]
        parts = parts.rearrange("p (u w k s) -> p u w k s", u=DEEP, w=2, k=PARTS)
        at = [0]

        def place(rows, *shape):
            n, lo = 1, at[0]
            for d in shape:
                n *= d
            at[0] = lo + n
            return route_sb[0:rows, lo:lo + n]

        y2 = place(P, NT, K2, ROW).rearrange("p (n k c) -> p n k c", n=NT, k=K2)
        over = place(1, E, B * S // TR).rearrange("p (e n) -> p e n", e=E)
        upto = place(1, E, E).rearrange("p (e n) -> p e n", e=E)
        past = place(1, TABLE, E).rearrange("p (t e) -> p t e", t=TABLE)
        past_n = place(1, TABLE, E).rearrange("p (t e) -> p t e", t=TABLE)
        yT_tile = xn.rearrange("p a n c -> p (a n c)")[:, 0:2 * TR].rearrange("p (a t) -> p a t", a=2)
        r_tile = rest.rearrange("p a w s -> p (a w s)")[:, 0:TQ * TH * C].rearrange("p (a h c) -> p a h c", a=TQ, h=TH)
        w1_cur = qk32.rearrange("p a w f -> p (a w) f")
        w2_cur = [op.rearrange("p j s -> p (j s)").bitcast(f32)[:, F * n:F * (n + 1)].rearrange("p (c n) -> p c n", c=FC)
                  for op in k_op[0:TQ // 2] for n in range(2)]
        hid = probs[:, 0:2, :, :]
        hid_tile = probs[:, 0, :, :].rearrange("p c s -> p (c s)")[:, 0:2 * FC * TR].rearrange("p (a c t) -> p a c t", a=2, c=FC)
        r_at = [probs[:, 2:4, :, :].rearrange("p x y s -> p (x y s)")[:, NT * K2 * C * n:NT * K2 * C * (n + 1)] for n in range(B // 2)]
        r_at += [op.rearrange("p j s -> p (j s)").bitcast(f32) for op in q_op]
        r_seq = [at.rearrange("p (n k c) -> p n k c", n=NT, k=K2) for at in r_at]
        y_tile = probs[:, 2, :, :].rearrange("p y s -> p (y s)")[:, 0:RING * TH * ROW].rearrange("p (u h c) -> p u h c", u=RING, h=TH)
        ps = ctx.enter_context(nc.psum_tensor("ps", [P, 8, 512], f32))

        s_w1st = sem("first_weights_loaded")
        s_wo, s_x, s_w, s_wffn = sem("wo_loaded"), [sem("x_loaded0"), sem("x_loaded1")], sem("weights_loaded"), sem("ffn_weights_loaded")
        s_const, s_idbf, s_pad = sem("constants_set"), sem("id_bf_set"), sem("padding_set")
        s_st, s_ve, s_rstd = sem("ln_steps"), sem("ln_var_eps"), sem("ln_rstd")
        s_xn, s_xnTp, s_xnT = sem("xn_ready"), sem("xnT_in_psum"), sem("xnT_ready")
        s_qp, s_kp, s_vp = sem("q_in_psum"), sem("k_in_psum"), sem("v_in_psum")
        s_qk32, s_hi, s_rest = sem("qk32_ready"), sem("first_parts_ready"), sem("rest_ready")
        s_mid, s_lo, s_v, s_scr = sem("second_parts_ready"), sem("third_parts_ready"), sem("v_stored"), [sem(f"scratch_stored{u}") for u in range(DEEP)]
        s_ld = [sem(f"qk_op_loaded{g}") for g in range(HG)]
        s_sh = [sem(f"shift_rows_loaded{g}") for g in range(HG)]
        s_sa, s_max = sem("row_scores_in_psum"), sem("row_maxima_taken")
        s_ms, s_msp, s_mxTp, s_mxT = sem("max_split_steps"), sem("max_parts_ready"), sem("mxT_in_psum"), sem("mxT_ready")
        s_sb, s_exp = sem("key_scores_in_psum"), sem("probs_ready")
        s_vop, s_pv = sem("v_op_ready"), sem("pv_key_tiles_done")
        s_ot, s_orec, s_onrm, s_o = sem("o_transposed"), sem("o_reciprocal"), sem("o_normalised"), sem("o_ready")
        s_xbo, s_ap, s_x2 = sem("x_plus_bias"), sem("attention_projected"), sem("x2_ready")
        s_y, s_yTp, s_yT = sem("y_rows_ready"), sem("yT_in_psum"), sem("yT_ready")
        s_lgp, s_rt, s_gd, s_ge = sem("logits_in_psum"), sem("router_steps"), sem("logit_differences"), sem("logit_exps")
        s_fillrows, s_sl, s_yn, s_bn = sem("filling_rows_set"), sem("slot_sums"), sem("y_ready"), sem("ln2_begun")
        s_l2, s_scale, s_nb = sem("ln2_steps"), sem("ln2_scales_ready"), sem("ln2_normalising")
        s_keep, s_kept = sem("keep_steps"), sem("yT_kept")
        s_rk, s_slot, s_tab = sem("ranks_in_psum"), sem("slots_ready"), sem("table_steps")
        s_put, s_fill, s_route = sem("slots_written"), sem("filling_written"), sem("routing_constants")
        s_up, s_gelu, s_dn, s_mix = sem("shared_up_in_psum"), sem("shared_hidden_ready"), sem("shared_down_in_psum"), sem("shared_added")
        s_yl = [sem(f"y_tile_loaded{u}") for u in range(RING)]
        s_tT, s_tyT, s_tup, s_th = sem("tile_T_in_psum"), sem("tile_yT_ready"), sem("tile_up_in_psum"), sem("tile_hidden_ready")
        s_tdn, s_w1c, s_w2c, s_rid = sem("tile_down_in_psum"), sem("tile_w1_ready"), sem("tile_w2_ready"), sem("tile_row_ids")
        s_rt2, s_res = sem("tile_result_ready"), [sem(f"results_written{u}") for u in range(TQ)]
        s_rl, s_gate, s_b2s, s_fin = [sem(f"results_loaded{u}") for u in range(B)], sem("gate_steps"), sem("shared_bias_added"), sem("combined")
        s_partp, s_finp = sem("pool_combine_steps"), sem("combined_by_pool")
        s_part, s_cn, s_cntp = sem("first_choice_added"), sem("slot_steps"), sem("counts_in_psum")
        s_go, s_out = sem("scatter_steps"), sem("stored")

        def wait(eng, s, n):
            if not (isinstance(n, int) and n <= 0):
                eng.wait_ge(s, n)

        def pairs(eng, body):
            with eng.Fori(0, B // 2 - 1) as it:
                body(it * 2, 0)
                body(it * 2 + 1, 1)
            body(B - 2, 0)
            body(B - 1, 1)

        def sequences(eng, body):
            body(0)
            with eng.Fori(1, B - 1) as b:
                body(b)
            body(B - 1)

        N_W1ST, N_W = 6, 8
        TILE_PARTS = (slice(0, 2 * NT), slice(2 * NT, B * NT))
        N_WFFN = 2 * NE + 2
        N_SCR = 6
        N_ROUTE = 9
        N_LD = 6
        XNT_ACT = (1, 2, 3)
        UP0, DN0 = 0, 4
        BK_TT, BK_TU, BK_TD = 0, 2, 6
        BK_S, BK_A, BK_O, BK_M = 0, 2, 6, 7

        PV_LAG, MX_STEP, YT_STEP = 11, 7, 13
        Y_STEPS = (-1, 3, 7, 11)
        ROW_TILES = ((0,), (1, 2), (3,), ())
        R, Q = 4, 2

        def e_tile(b, i):
            return b * NT + i

        def key_banks(b, hg):
            return J if isinstance(b, int) and b == B - 1 and hg >= HG - 2 else 2

        N_MAT = 4
        L2 = 9
        N_PAD = 6
        N_PADS, N_TAB = 2, N_MAT + 13

        BY_DVE = tuple(b for b in range(B) if b not in BY_POOL)

        ORDER = [("shared" if c == "s" else "routed", int(b)) for c, b in "r0 s4 r1 r4 s5 r5 r6 s6 r7 s7".split()]

        block = ctx.enter_context(nc.Block())

        @block.sync
        def _(sp):
            by_tile = x.rearrange("(n p) c -> p n c", p=P)
            first, others = TILE_PARTS
            sp.dma_start(x_sb[:, first, :], by_tile[:, first, :]).then_inc(s_x[0], 16)
            for dst, src in ((id_sb, ident), (wq_sb, WqT), (wk_sb, WkT)):
                sp.dma_start(dst[:, :], src).then_inc(s_w1st, 16)
            for dst, src in ((bq_sb, bq), (bk_sb, bk)):
                sp.dma_start(dst[:, :], src.rearrange("(c o) -> c o", o=1)).then_inc(s_w1st, 16)
            sp.dma_start(wv_sb[:, :], WvT).then_inc(s_w1st, 16)
            sp.dma_start(x_sb[:, others, :], by_tile[:, others, :]).then_inc(s_x[1], 16)
            for dst, src in ((bv_sb, bv), (bo_sb, bo)):
                sp.dma_start(dst[:, :], src.partition_broadcast(P)).then_inc(s_w, 16)
            sp.dma_start(iota_sb[:, :], iota8).then_inc(s_w, 16)
            for j in range(J):
                m = head_mask.rearrange("(g j) -> j g", j=J)[j, :].partition_broadcast(32)
                with nc.allow_non_contiguous_dma(reason="16 values"):
                    sp.dma_start(mask_sb[32 * j:32 * j + 32, :], m).then_inc(s_w, 16)
            sp.dma_start(wr_sb[:, :], Wr).then_inc(s_w, 16)
            for j in range(J):
                src = WoT.rearrange("(g j d) n -> j g d n", g=HG, j=J)[j]
                sp.dma_start(wo_sb[32 * j:32 * j + 32, :], src).then_inc(s_wo, 16)
            for dst, src in ((tri_f, tri), (reg_f, region_at), (thr_sb, thresholds), (tid_sb, tile_ids), (regr_sb, region_row), (tslot_sb, tile_slots)):
                sp.dma_start(dst[:, :], src).then_inc(s_route, 16)
            sp.dma_start(tri8_sb[:, :, :], tri8).then_inc(s_route, 16)
            sp.dma_start(ids_sb[:, :, :], row_ids.rearrange("(n p) k -> p n k", p=P)).then_inc(s_route, 16)
            sp.dma_start(dump_sb[:, :, :, :], dump_ids).then_inc(s_route, 16)

            def store_parts(b, u):
                sp.wait_ge(s_mid, 2 * b + 2)
                sp.wait_ge(s_lo, 2 * b + 2)
                sp.dma_start(q_scr[b, :, :], parts[:, u, 0, :, :]).then_inc(s_scr[u], 16)
                for r in range(PARTS):
                    for lo, hi, at in ((r, PARTS, 0), (0, r, PARTS - r)):
                        if hi > lo:
                            sp.dma_start(k_scr[r][b, :, at * S:(at + hi - lo) * S],
                                         parts[:, u, 1, lo:hi, :]).then_inc(s_scr[u], 16)

            def load_group(b, hg):
                wait(sp, s_sb, (b * HG + hg - HG + 1) * (J * NT))
                for r in range(PARTS):
                    for scr, op in ((q_scr, q_op), (k_scr[r], k_op)):
                        src = scr[b, J * D * hg:J * D * (hg + 1), :]
                        src = src.rearrange("(h d) (a t) -> (d a) h t", d=D, a=PARTS)
                        sp.dma_start(op[hg][PR * r:PR * (r + 1), :, :], src).then_inc(s_ld[hg], 16)

            def load_shift(b, hg):
                g = b * HG + hg
                sp.wait_ge(s_mxT, g + 1)
                for a in range(SHIFTS):
                    n = J * NT
                    sp.dma_start(q_op[hg][SH + a:SH + a + 1, :, :].rearrange("o j (n t) -> o (j n) t", t=P),
                                 mxT[n * a:n * (a + 1), hg % 2, :]).then_inc(s_sh[hg], 16)

            for b in range(B):
                store_parts(b, b % DEEP)
                if b == DEEP - 1:
                    sp.wait_ge(s_const, 3 * HG)
                    sp.wait_ge(s_scr[0], 16 * N_SCR)
                    load_group(0, 0)
                elif b == DEEP + 1:
                    load_group(0, 1)
            load_group(0, 2)
            for u in range(DEEP):
                sp.wait_ge(s_scr[u], (B // DEEP) * (16 * N_SCR))
            load_shift(0, 0)

            sp.wait_ge(s_route, 16 * N_ROUTE)

            sp.wait_ge(s_pad, N_PAD)
            for n in range(E):
                to = slots[E * REGION + TR * n:E * REGION + TR * (n + 1), :].rearrange("(h p) c -> p h c", p=P)
                sp.dma_start(to[:, :, 0:C], zero_sb[:, :, :]).then_inc(s_fill, 16)
                with nc.allow_non_contiguous_dma(reason="row numbers"):
                    sp.dma_start(to[:, :, C:ROW].bitcast(u32), dump_sb[:, E + n, :, :]).then_inc(s_fill, 16)


            def load_experts(hg):
                if hg == 0:
                    sp.dma_start(b2_sb[:, :, :], b2.partition_broadcast(P)).then_inc(s_wffn, 16)
                    sp.dma_start(b1_sb[:, :, :], b1).then_inc(s_wffn, 16)
                for e in range(hg, NE, HG):
                    sp.dma_start(w1_sb[:, e, :], W1[:, e, :]).then_inc(s_wffn, 16)
                    sp.dma_start(w2_sb[:, e, :, :], W2[:, e, :, :]).then_inc(s_wffn, 16)

            def feed(b):
                first, last = isinstance(b, int) and b == 0, isinstance(b, int) and b == B - 1
                for hg in range(HG):
                    if hg == 0:
                        load_group(b, HG - 1)
                    elif not last:
                        load_group(b + 1, hg - 1)
                    if hg < HG - 1:
                        load_shift(b, hg + 1)
                    elif not last:
                        load_shift(b + 1, 0)
                    if first:
                        load_experts(hg)

            sequences(sp, feed)

            sp.wait_ge(s_tab, N_MAT + N_PADS)
            sp.wait_ge(s_fillrows, 1)
            pad_regs = [sp.alloc_register(f"pad{e}") for e in range(E)]
            sp.load(pad_regs, pad_row[0:1, :])
            for e in range(E):
                at = sp.snap(pad_regs[e], min_val=0, max_val=E * REGION - TR)
                sp.dma_start(slots[bass.ds(at, TR), :].rearrange("(h p) c -> p h c", p=P), fill_sb[:, e, :, :]).then_inc(s_fill, 16)
            sp.wait_ge(s_tab, N_TAB)
            sp.wait_ge(s_exp, NG * J * NT)
            sp.wait_ge(s_pv, NG * NT)
            sp.wait_ge(s_put, B * (16 * NC))
            sp.wait_ge(s_fill, 16 * (3 * E))
            row_regs = [sp.alloc_register(f"row{u}") for u in range(RING)]

            def load_tiles(it, n=RING):
                sp.load(row_regs, tab_row[0:1, bass.ds(it * RING, RING)])
                for u in range(n):
                    t = it * RING + u
                    at = sp.snap(row_regs[u], min_val=0, max_val=E * REGION + (E - 1) * TR)
                    wait(sp, s_rid, t - RING + 1)
                    wait(sp, s_tT, t - RING + 1)
                    sp.dma_start(y_tile[:, u, :, :], slots[bass.ds(at, TR), :].rearrange("(h p) c -> p h c", p=P)).then_inc(s_yl[u], 16)

            load_tiles(0)
            with sp.Fori(1, TABLE // RING - 1) as it:
                load_tiles(it)
            load_tiles(TABLE // RING - 1, TILES - TABLE + RING)

            for v in range(TQ):
                sp.wait_ge(s_res[v], len(range(v, TILES, TQ)) * (16 * TH))
            sp.wait_ge(s_rid, TILES)
            sp.wait_ge(s_tT, TILES)
            by_seq = results[0:K2 * B * S, :].rearrange("(n p k) c -> p n k c", p=P, k=K2)

            for b in range(B):
                sp.dma_start(r_seq[b], by_seq[:, NT * b:NT * (b + 1), :, :]).then_inc(s_rl[b], 16)
            for b in range(B):
                if b in BY_POOL:
                    sp.wait_ge(s_finp, BY_POOL.index(b) + 1)
                else:
                    sp.wait_ge(s_fin, BY_DVE.index(b) + 1)
                if b >= EARLY:
                    sp.wait_ge(s_mix, b + 1)
                sp.dma_start(out.rearrange("(n p) c -> p n c", p=P)[:, NT * b:NT * (b + 1), :],
                             x_sb[:, NT * b:NT * (b + 1), :]).then_inc(s_out, 16)
            sp.wait_ge(s_out, 16 * B)

        @block.gpsimd
        def _(pool):
            def zero_scores(hg):
                for op in (q_op, k_op):
                    nc.gpsimd.memset(op[hg][:, :, :].bitcast(f32), 0.0).then_inc(s_const, 1)

            def ln1_rstd(n):
                some = slice(2 * NT * n, 2 * NT * (n + 1))
                pool.wait_ge(s_ve, n + 1)
                nc.gpsimd.tensor_tensor(rstd[:, some], var_eps[:, some], neg_half[:, some], ALU.pow).then_inc(s_rstd, 1)

            def third_parts(b):
                for w in range(2):
                    pool.wait_ge(s_mid, 2 * b + w + 1)
                    nc.gpsimd.tensor_tensor(parts[:, b % DEEP, w, 2, :], rest[:, b % 2, w, :], parts[:, b % DEEP, w, 1, :],
                                            ALU.subtract).then_inc(s_lo, 1)

            nc.gpsimd.memset(neg_half[:, :], -0.5).then_inc(s_pad, 1)
            for hg in range(HG - 1):
                zero_scores(hg)
            pool.wait_ge(s_pad, 1)
            pool.wait_ge(s_const, 2 * (HG - 1))
            ln1_rstd(0)
            zero_scores(HG - 1)
            nc.gpsimd.memset(v_op[:, :, :, :, :], 0.0).then_inc(s_pad, 1)
            ln1_rstd(1)
            pool.wait_ge(s_const, 2 * HG)
            pool.wait_ge(s_pad, 2)
            pool.wait_ge(s_rstd, 2)
            for hg in range(HG):
                nc.gpsimd.memset(k_op[hg][SH:P, :, :].bitcast(f32), TWO_MINUS_ONES).then_inc(s_const, 1)
            pool.wait_ge(s_const, 3 * HG)
            ln1_rstd(2)
            third_parts(0)
            third_parts(1)
            ln1_rstd(3)
            nc.gpsimd.memset(v_op[:, :, :, :, 0:1], 1.0).then_inc(s_pad, 1)
            nc.gpsimd.memset(zero_sb[:, :, :], 0.0).then_inc(s_pad, 1)
            nc.gpsimd.memset(e_const[:, :], 2.718281828459045).then_inc(s_pad, 1)
            nc.gpsimd.memset(quarter[:, :], 0.25).then_inc(s_pad, 1)
            pool.wait_ge(s_pad, N_PAD)
            for b in range(2, B):
                third_parts(b)
            pool.wait_ge(s_v, B)

            def gather_v(b, hg):
                wait(pool, s_pv, NT * (b * HG + hg - HG + 1))
                src = v_all[:, b, :, J * D * hg:J * D * (hg + 1)].rearrange("p n (j d) -> p n j d", j=J)
                nc.gpsimd.tensor_copy(v_op[:, hg, :, :, 1:1 + D], src).then_inc(s_vop, 1)

            def ln2_scales(b):
                some, n = slice(0, NT), b * L2
                even, odd = stats[:, some, 0:3], stats[:, some, 3:6]
                pool.wait_ge(s_st, (B // 2) * 7 + b + 1)
                wait(pool, s_yn, b)
                nc.gpsimd.tensor_tensor(mean_d[:, some], even[:, :, 1], odd[:, :, 1], ALU.subtract).then_inc(s_l2, 1)
                nc.gpsimd.tensor_tensor(mean[:, some], even[:, :, 1], odd[:, :, 1], ALU.add).then_inc(s_l2, 1)
                nc.gpsimd.tensor_tensor(dev[:, some], even[:, :, 2], odd[:, :, 2], ALU.add).then_inc(s_l2, 1)
                pool.wait_ge(s_l2, n + 3)
                nc.gpsimd.tensor_tensor(mean_d2[:, some], mean_d[:, some], mean_d[:, some], ALU.mult).then_inc(s_l2, 1)
                nc.gpsimd.tensor_scalar(neg_mean[:, :], mean[:, some], -0.5, None, ALU.mult).then_inc(s_l2, 1)
                nc.gpsimd.tensor_scalar(dev[:, some], dev[:, some], 1.0 / C, EPS, ALU.mult, ALU.add).then_inc(s_l2, 1)
                pool.wait_ge(s_l2, n + 6)
                nc.gpsimd.tensor_tensor(mean_d2q[:, :], mean_d2[:, some], quarter[:, :], ALU.mult).then_inc(s_l2, 1)
                pool.wait_ge(s_l2, n + 7)
                nc.gpsimd.tensor_tensor(var_eps[:, some], mean_d2q[:, :], dev[:, some], ALU.add).then_inc(s_l2, 1)
                pool.wait_ge(s_l2, n + 8)
                nc.gpsimd.tensor_tensor(rstd[:, some], var_eps[:, some], neg_half[:, some], ALU.pow).then_inc(s_l2, 1)
                pool.wait_ge(s_l2, n + 9)
                nc.gpsimd.tensor_tensor(neg_shift[:, :], neg_mean[:, :], rstd[:, some], ALU.mult).then_inc(s_scale, 1)

            def keep_yT(b):
                pool.wait_ge(s_yT, b + 1)
                pool.sem_inc(s_keep, 1)
                nc.gpsimd.tensor_copy(yT[:, b, :], yT_now[:, :]).then_inc(s_kept, 1)

            def put_rows(b):
                pool.wait_ge(s_slot, b + 1)
                pool.sem_inc(s_go, 1)
                for i in range(NT):
                    for k in range(K2):
                        nc.gpsimd.indirect_dma_start(slots, bass.IndirectOffsetOnAxis(slot_u[:, K2 * i + k:K2 * i + k + 1], 0),
                                                     y2[:, i, k, :], None).then_inc(s_put, 16)

            gather_v(0, 0)
            gather_v(0, 1)

            pool.wait_ge(s_xn, B)
            with pool.Fori(0, B) as b:
                sl = x_sb[:, bass.ds(b * NT, NT), :]
                nc.gpsimd.tensor_tensor(sl, sl, bo_sb[:, :].unsqueeze(1).to_broadcast([P, NT, C]), ALU.add).then_inc(s_xbo, 1)

            pool.wait_ge(s_route, 16 * N_ROUTE)
            nc.gpsimd.memset(fill_sb[:, :, :, 0:C], 0.0)
            nc.gpsimd.tensor_copy(fill_sb[:, :, :, C:ROW].bitcast(u32), dump_sb[:, 0:E, :, :]).then_inc(s_fillrows, 1)

            def gather_and_route(b):
                first, last = isinstance(b, int) and b == 0, isinstance(b, int) and b == B - 1
                gather_v(b, 2)
                if not first:
                    ln2_scales(b - 1)
                gather_v(b, 3)
                if not last:
                    gather_v(b + 1, 0)
                    gather_v(b + 1, 1)
                if not first:
                    keep_yT(b - 1)
                    put_rows(b - 1)

            sequences(pool, gather_and_route)
            ln2_scales(B - 1)
            keep_yT(B - 1)
            put_rows(B - 1)
            pool.wait_ge(s_gd, B)
            nc.gpsimd.tensor_tensor(l_exp[:, :], e_const[:, :], l_diff[:, :], ALU.pow).then_inc(s_ge, 1)

            def put_results(t, v):
                pool.wait_ge(s_rt2, t + 1)
                pool.sem_inc(s_go, 1)
                for h in range(TH):
                    nc.gpsimd.indirect_dma_start(results, bass.IndirectOffsetOnAxis(row_id[:, v, h:h + 1], 0),
                                                 r_tile[:, v, h, :], None).then_inc(s_res[v], 16)

            with pool.Fori(0, TILES // TQ) as it:
                for v in range(TQ):
                    put_results(it * TQ + v, v)
            for t in range(TILES // TQ * TQ, TILES):
                put_results(t, t % TQ)

            pool.wait_ge(s_gate, 3)
            pool.wait_ge(s_mix, EARLY)
            for n, b in enumerate(BY_POOL):
                some, r = slice(NT * b, NT * (b + 1)), r_seq[b]
                gates = top_p[:, :, some].rearrange("p k n -> p n k").unsqueeze(3).to_broadcast([P, NT, K2, C])
                pool.wait_ge(s_rl[b], 16)
                nc.gpsimd.tensor_tensor(r, r, gates, ALU.mult).then_inc(s_partp, 1)
                pool.wait_ge(s_partp, 2 * n + 1)
                nc.gpsimd.tensor_tensor(r[:, :, 0, :], r[:, :, 0, :], r[:, :, 1, :], ALU.add).then_inc(s_partp, 1)
                pool.wait_ge(s_partp, 2 * n + 2)
                nc.gpsimd.tensor_tensor(x_sb[:, some, :], x_sb[:, some, :], r[:, :, 0, :], ALU.add).then_inc(s_finp, 1)

        @block.scalar
        def _(act):
            act.wait_ge(s_w1st, 16 * N_W1ST)

            def copy_xnT(b, par):
                act.wait_ge(s_xnTp, b + 1)
                wait(act, s_vp, b - 1)
                nc.scalar.activation(xnT[:, par, :], ps[:, par, :], ACT.Copy).then_inc(s_xnT, 1)

            def first_parts(b, par, u, it):
                for w, (ready, bias) in enumerate(((s_qp, bq_sb), (s_kp, bk_sb))):
                    act.wait_ge(ready, b + 1)
                    wait(act, s_rest, 2 * (b - 2) + w + 1)
                    nc.scalar.activation(qk32[:, par, w, :], ps[:, 2 + 2 * w + par, :], ACT.Identity,
                                         bias=bias[:, 0:1]).then_inc(s_qk32, 1)
                    act.wait_ge(s_qk32, 2 * b + w + 1)
                    wait(act, s_scr[u], it * (16 * N_SCR))
                    nc.scalar.activation(parts[:, u, w, 0, :], qk32[:, par, w, :], ACT.Copy).then_inc(s_hi, 1)

            def second_parts(b, par, u):
                for w in range(2):
                    act.wait_ge(s_rest, 2 * b + w + 1)
                    nc.scalar.activation(parts[:, u, w, 1, :], rest[:, par, w, :], ACT.Copy).then_inc(s_mid, 1)

            def split(b, par, u, it):
                first_parts(b, par, u, it)
                if b + 1 in XNT_ACT:
                    copy_xnT(b + 1, 1 - par)
                if not (isinstance(b, int) and b == 0):
                    second_parts(b - 1, 1 - par, (u - 1) % DEEP)

            for u in range(DEEP):
                split(u, u % 2, u, 0)
            for u in range(DEEP):
                split(B - DEEP + u, u % 2, u, 1)
            second_parts(B - 1, 1, DEEP - 1)

            def ln2_normalise(b, i):
                if i == 0:
                    act.wait_ge(s_scale, b + 1)
                    wait(act, s_put, b * (16 * NC))
                    wait(act, s_yTp, b)
                    act.sem_inc(s_nb, 1)
                last = nc.scalar.activation(y2[:, i, :, 0:C], x_sb[:, e_tile(b, i), :].unsqueeze(1).to_broadcast([P, K2, C]),
                                            ACT.Identity, bias=neg_shift[:, i:i + 1], scale=rstd[:, i:i + 1])
                if i == NT - 1:
                    last.then_inc(s_yn, 1)

            def copy_yT(b):
                act.wait_ge(s_yTp, b + 1)
                wait(act, s_lgp, b)
                wait(act, s_kept, b)
                nc.scalar.activation(yT_now[:, :], ps[:, BK_M, :], ACT.Copy).then_inc(s_yT, 1)

            def max_out(b, hg):
                g = b * HG + hg
                act.wait_ge(s_mxTp, g + 1)
                if hg >= 2:
                    act.wait_ge(s_sh[hg - 2], (b + 1) * (16 * SHIFTS))
                else:
                    wait(act, s_sh[hg + 2], b * (16 * SHIFTS))
                nc.scalar.activation(mxT[:, hg % 2, :], ps[0:SHIFTS * J * NT, BK_M, 0:P // 2].bitcast(bf16), ACT.Copy).then_inc(s_mxT, 1)

            max_out(0, 0)

            def exps(b):
                first, last_b = isinstance(b, int) and b == 0, isinstance(b, int) and b == B - 1
                for hg in range(HG):
                    g = b * HG + hg
                    for i in range(NT):
                        wait(act, s_pv, (g - 1) * NT + i + 1)
                        for j in range(J):
                            n = g * (J * NT) + i * J + j
                            act.wait_ge(s_sb, n + 1)
                            nc.scalar.activation(probs[:, i, j, :], ps[:, BK_S + j % key_banks(b, hg), :],
                                                 ACT.Exp, scale=float(D) ** -0.5).then_inc(s_exp, 1)
                            if i * J + j == MX_STEP:
                                if hg < HG - 1:
                                    max_out(b, hg + 1)
                                elif not last_b:
                                    max_out(b + 1, 0)
                            step = (hg - 2) * J * NT + i * J + j
                            if step in Y_STEPS and not first:
                                ln2_normalise(b - 1, Y_STEPS.index(step))
                            if step == YT_STEP + 2 and not first:
                                copy_yT(b - 1)

            sequences(act, exps)

            act.wait_ge(s_wffn, 16 * N_WFFN)
            act.wait_ge(s_pv, NG * NT)

            def gelus(b):
                par = b % 2
                for c in range(FC):
                    act.wait_ge(s_up, b * FC + c + 1)
                    if c == 0:
                        wait(act, s_dn, b - 1)
                    nc.scalar.activation(hid[:, par, c, :], ps[:, UP0 + c, :], ACT.Gelu_apprx_tanh,
                                         bias=b1_sb[:, E, c:c + 1]).then_inc(s_gelu, 1)

            gelus(0)
            for i in range(NT):
                ln2_normalise(B - 1, i)
            copy_yT(B - 1)
            for b in range(1, EARLY):
                gelus(b)

            act.wait_ge(s_dn, EARLY)

            def tile_gelus(t, v):
                par = v % 2
                act.wait_ge(s_w1c, t + 1)
                for c in range(FC):
                    if c % 2 == 0:
                        act.wait_ge(s_tup, t * (FC // 2) + c // 2 + 1)
                    if c == 0:
                        wait(act, s_tdn, t - 1)
                    nc.scalar.activation(hid_tile[:, par, c, :], ps[:, BK_TU + 2 * par + c // 2, TR * (c % 2):TR * (c % 2 + 1)],
                                         ACT.Gelu_apprx_tanh, bias=b1_cur[:, v, c:c + 1]).then_inc(s_th, 1)

            for u in range(RING):
                tile_gelus(u, u % TQ)
            with act.Fori(1, TILES // RING) as it:
                for u in range(RING):
                    tile_gelus(it * RING + u, u % TQ)
            for t in range(TILES // RING * RING, TILES):
                tile_gelus(t, t % TQ)

            act.wait_ge(s_tdn, TILES)
            for b in range(EARLY, B):
                gelus(b)

        @block.vector
        def _(dve):
            nc.vector.memset(mx_parts[:, :], 0.0).then_inc(s_idbf, 1)

            def moments(some, steps, at, part):
                even, odd = stats[:, some, 0:3], stats[:, some, 3:6]
                if part == 0:
                    dve.wait_ge(steps, at)
                    nc.vector.tensor_tensor(mean_d[:, some], even[:, :, 1], odd[:, :, 1], ALU.subtract).then_inc(steps, 1)
                    nc.vector.tensor_tensor(mean[:, some], even[:, :, 1], odd[:, :, 1], ALU.add).then_inc(steps, 1)
                    nc.vector.tensor_tensor(dev[:, some], even[:, :, 2], odd[:, :, 2], ALU.add).then_inc(steps, 1)
                elif part == 1:
                    dve.wait_ge(steps, at + 3)
                    nc.vector.tensor_tensor(mean_d2[:, some], mean_d[:, some], mean_d[:, some], ALU.mult).then_inc(steps, 1)
                    nc.vector.tensor_scalar(mean[:, some], mean[:, some], 0.5, None, ALU.mult).then_inc(steps, 1)
                    nc.vector.tensor_scalar(dev[:, some], dev[:, some], 1.0 / C, EPS, ALU.mult, ALU.add).then_inc(steps, 1)
                else:
                    dve.wait_ge(steps, at + 6)
                    nc.vector.scalar_tensor_tensor(out=var_eps[:, some], in0=mean_d2[:, some], scalar=0.25, in1=dev[:, some],
                                                   op0=ALU.mult, op1=ALU.add).then_inc(s_ve, 1)

            def ln1(n):
                some = slice(2 * NT * n, 2 * NT * (n + 1))
                if n < 2:
                    dve.wait_ge(s_x[n], 16)
                for t in range(some.start, some.stop):
                    last = nc.vector.bn_stats(stats[:, t, :], x_sb[:, t, :])
                last.then_inc(s_st, 1)
                for part in range(3):
                    moments(some, s_st, 7 * n + 1, part)

            def normalise(b, par):
                dve.wait_ge(s_rstd, b // 2 + 1)
                wait(dve, s_xnTp, b - 1)
                for i in range(NT):
                    t = e_tile(b, i)
                    last = nc.vector.tensor_scalar(xn[:, par, i, :], x_sb[:, t, :], mean[:, t:t + 1], rstd[:, t:t + 1],
                                                   ALU.subtract, ALU.mult)
                last.then_inc(s_xn, 1)

            def copy_xnT(b, par):
                dve.wait_ge(s_xnTp, b + 1)
                wait(dve, s_vp, b - 1)
                nc.vector.tensor_copy(xnT[:, par, :], ps[:, par, :]).then_inc(s_xnT, 1)

            def store_v(b, par):
                dve.wait_ge(s_vp, b + 1)
                nc.vector.tensor_tensor(v_all[:, b, :, :], ps[:, 6 + par, :].rearrange("p (n c) -> p n c", c=C),
                                        bv_sb[:, :].unsqueeze(1).to_broadcast([P, NT, C]), ALU.add).then_inc(s_v, 1)

            def take_rest(b, w):
                dve.wait_ge(s_hi, 2 * b + w + 1)
                wait(dve, s_lo, 2 * (b - 2) + w + 1)
                nc.vector.tensor_tensor(rest[:, b % 2, w, :], qk32[:, b % 2, w, :], parts[:, b % DEEP, w, 0, :],
                                        ALU.subtract).then_inc(s_rest, 1)

            ln1(0)
            normalise(0, 0)
            normalise(1, 1)
            copy_xnT(0, 0)
            ln1(1)
            for b in range(B):
                if b + 1 < B and b + 1 not in XNT_ACT:
                    copy_xnT(b + 1, 1 - b % 2)
                if b in (0, 2):
                    ln1(2 + b // 2)
                if b + 2 < B:
                    normalise(b + 2, b % 2)
                take_rest(b, 0)
                take_rest(b, 1)
                if b == 0:
                    dve.wait_ge(s_w, 16 * N_W)
                    nc.vector.tensor_copy(id_bf[:, :], id_sb[:, :]).then_inc(s_idbf, 1)
                store_v(b, b % 2)

            PAIRS = J * NT // 2

            def row_max(g, p, slot):
                dve.wait_ge(s_sa, g * PAIRS + p + 1)
                bank = BK_A + 2 * (p % 2)
                nc.vector.reduce_max(mx[:, slot % 2, 2 * p:2 * p + 2], ps[:, bank:bank + 2, :], AX.X).then_inc(s_max, 1)

            def max_split(g, slot, step):
                m = mx[:, slot % 2, :]
                if step == 0:
                    dve.wait_ge(s_max, (g + 1) * PAIRS)
                    wait(dve, s_mxTp, g)
                    nc.vector.tensor_copy(mx_parts[:, 0:J * NT], m).then_inc(s_ms, 1)
                else:
                    dve.wait_ge(s_ms, g + 1)
                    nc.vector.tensor_tensor(mx_parts[:, J * NT:2 * J * NT], m, mx_parts[:, 0:J * NT], ALU.subtract).then_inc(s_msp, 1)

            def out_norm(b, hg, step):
                g = b * HG + hg
                if step == 0:
                    wait(dve, s_onrm, g)
                    dve.wait_ge(s_pv, (g + 1) * NT)
                    nc.vector.transpose(o_t[:, :, :].rearrange("p a c -> p (a c)"), ps[:, BK_O, :]).then_inc(s_ot, 1)
                elif step == 1:
                    dve.wait_ge(s_ot, g + 1)
                    nc.vector.reciprocal(o_rec[:, :], o_t[:, :, 0]).then_inc(s_orec, 1)
                elif step == 2:
                    dve.wait_ge(s_orec, g + 1)
                    if hg == 0:
                        wait(dve, s_o, b)
                    nc.vector.scalar_tensor_tensor(out=o_all[:, :, hg, :], in0=o_t[:, :, 1:1 + D],
                                                   scalar=mask_sb[:, hg:hg + 1],
                                                   in1=o_rec[:, :].unsqueeze(2).to_broadcast([P, S // 32, D]),
                                                   op0=ALU.mult, op1=ALU.mult).then_inc(s_onrm, 1)
                elif hg == HG - 1:
                    dve.wait_ge(s_onrm, g + 1)
                    wait(dve, s_ap, b)
                    nc.vector.transpose(o_sb[:, :], o_all[:, :, :, :].rearrange("p a g d -> p (a g d)")).then_inc(s_o, 1)

            def residual(b):
                if isinstance(b, int) and b == 0:
                    dve.wait_ge(s_xbo, B)
                dve.wait_ge(s_ap, b + 1)
                sl = x_sb[:, bass.ds(b * NT, NT), :]
                nc.vector.tensor_tensor(sl, ps[:, BK_M, :].rearrange("p (n c) -> p n c", c=C), sl, ALU.add).then_inc(s_x2, 1)

            def ln2_stats(b):
                dve.wait_ge(s_x2, b + 1)
                dve.sem_inc(s_bn, 1)
                for i in range(NT):
                    last = nc.vector.bn_stats(stats[:, i, :], x_sb[:, e_tile(b, i), :])
                last.then_inc(s_st, 1)

            def y_row_ids(b):
                wait(dve, s_put, b * (16 * NC))
                dve.sem_inc(s_bn, 1)
                nc.vector.tensor_copy(y2[:, :, :, C].bitcast(u32), ids_sb[:, bass.ds(b * NT, NT), :]).then_inc(s_y, 1)

            def router_step(b, step):
                if step == 0:
                    dve.wait_ge(s_lgp, b + 1)
                    nc.vector.tensor_copy(logits[:, :, :], ps[:, BK_M, 0:NT * E].rearrange("p (n e) -> p n e", e=E)).then_inc(s_rt, 1)
                elif step == 1:
                    dve.wait_ge(s_rt, b * R + 1)
                    dve.sem_inc(s_bn, 1)
                    for i in range(NT):
                        last = nc.vector.max(top8[:, i, :], logits[:, i, :])
                    last.then_inc(s_rt, 1)
                elif step == 2:
                    dve.wait_ge(s_rt, b * R + 2)
                    nc.vector.tensor_tensor(l_diff[:, bass.ds(b * NT, NT)], top8[:, :, 1], top8[:, :, 0], ALU.subtract).then_inc(s_gd, 1)
                    for i in range(NT):
                        last = nc.vector.max_index(top_i[:, i, :], top8[:, i, :], logits[:, i, :])
                    last.then_inc(s_rt, 1)
                else:
                    dve.wait_ge(s_rt, b * R + 3)
                    wait(dve, s_rk, b)
                    nc.vector.tensor_tensor(chosen[:, :, :].rearrange("p (n k) e -> p n k e", k=K2),
                                            iota_sb[:, :].unsqueeze(1).unsqueeze(1).to_broadcast([P, NT, K2, E]),
                                            top_i[:, :, 0:K2].unsqueeze(3).to_broadcast([P, NT, K2, E]),
                                            ALU.is_equal).then_inc(s_rt, 1)

            def slot_step(b, step):
                if step == 0:
                    dve.wait_ge(s_rk, b + 1)
                    nc.vector.tensor_tensor(at_f[:, :, :], ps[:, BK_M, 0:NC * E].rearrange("p (c e) -> p c e", e=E),
                                            chosen[:, :, :], ALU.mult).then_inc(s_sl, 1)
                else:
                    dve.wait_ge(s_sl, b + 1)
                    with nc.allow_low_precision(reason="whole numbers, one of them not zero"):
                        nc.vector.reduce_sum(slot_u[:, :], at_f[:, :, :], AX.X).then_inc(s_slot, 1)

            def count_step(b, step):
                if step == 0:
                    dve.wait_ge(s_rt, (b + 1) * R)
                    nc.vector.reduce_sum(seq_n[:, :], chosen[:, :, :].rearrange("p c e -> p e c"), AX.X).then_inc(s_cn, 1)
                else:
                    dve.wait_ge(s_cn, (b + 1) * Q + 1)
                    dve.wait_ge(s_sl, b + 1)
                    nc.vector.tensor_tensor(run_bf[:, :], run_bf[:, :], seq_n[:, :], ALU.add).then_inc(s_cn, 1)

            for p in range(PAIRS):
                row_max(0, p, 0)
            for p in range(PAIRS):
                row_max(1, p, 1)
                if p == 0:
                    for step in range(2):
                        max_split(0, 0, step)

            dve.wait_ge(s_route, 16 * N_ROUTE)
            nc.vector.tensor_copy(tri_bf[:, :], tri_f[:, :]).then_inc(s_tab, 1)
            nc.vector.tensor_copy(reg_bf[:, :], reg_f[:, :]).then_inc(s_tab, 1)
            nc.vector.memset(ones_bf[:, :], 1.0).then_inc(s_tab, 1)
            nc.vector.memset(tab_e[:, :], 0).then_inc(s_tab, 1)
            nc.vector.memset(run_bf[:, :], 0.0).then_inc(s_cn, Q)
            dve.wait_ge(s_tab, N_MAT)
            dve.wait_ge(s_cn, Q)

            def attend(b):
                first, last = isinstance(b, int) and b == 0, isinstance(b, int) and b == B - 1
                for hg in range(HG):
                    g = b * HG + hg
                    ahead = not last or hg < HG - 2
                    nxt = not last or hg < HG - 1
                    for p in range(PAIRS):
                        if nxt and p < 2:
                            max_split(g + 1, hg + 1, p)
                        if ahead:
                            row_max(g + 2, p, hg)
                        if 3 <= p < 7 and hg > 0:
                            out_norm(b, hg - 1, p - 3)
                        elif 3 <= p < 7 and not first:
                            out_norm(b - 1, HG - 1, p - 3)
                        if not first:
                            if hg == 1:
                                if p == 1:
                                    residual(b - 1)
                                if p == 3:
                                    ln2_stats(b - 1)
                            if hg == 2:
                                if p == 1:
                                    y_row_ids(b - 1)
                            if hg == 3:
                                if p in (1, 2, 4, 5):
                                    router_step(b - 1, (1, 2, 4, 5).index(p))
                                if p == 6:
                                    count_step(b - 1, 0)
                                if p == 7:
                                    slot_step(b - 1, 0)
                                    count_step(b - 1, 1)
                                    slot_step(b - 1, 1)
            sequences(dve, attend)
            for step in range(4):
                out_norm(B - 1, HG - 1, step)
            residual(B - 1)

            ln2_stats(B - 1)
            y_row_ids(B - 1)
            for step in range(4):
                router_step(B - 1, step)

            def add_shared(b):
                dve.wait_ge(s_dn, b + 1)
                sl = x_sb[:, NT * b:NT * (b + 1), :]
                nc.vector.tensor_tensor(sl, ps[:, DN0 + b % 2, :].rearrange("p (n c) -> p n c", c=C), sl, ALU.add).then_inc(s_mix, 1)

            add_shared(0)
            count_step(B - 1, 0)
            slot_step(B - 1, 0)
            count_step(B - 1, 1)
            slot_step(B - 1, 1)

            def step(n, instruction):
                instruction.then_inc(s_tab, 1)
                dve.wait_ge(s_tab, N_MAT + n)

            n_thr = B * S // TR
            dve.wait_ge(s_cntp, 1)
            step(1, nc.vector.tensor_copy(cnt[:, :], ps[0:1, BK_M, 0:E]))
            step(2, nc.vector.tensor_tensor(pad_row[:, :], cnt[:, :], regr_sb[:, :], ALU.add))
            step(3, nc.vector.tensor_tensor(over[:, :, :], cnt[:, :].unsqueeze(2).to_broadcast([1, E, n_thr]),
                                            thr_sb[:, :].unsqueeze(1).to_broadcast([1, E, n_thr]), ALU.is_gt))
            step(4, nc.vector.reduce_sum(n_tiles[:, :], over[:, :, :], AX.X))
            step(5, nc.vector.tensor_tensor(upto[:, :, :], n_tiles[:, :].unsqueeze(1).to_broadcast([1, E, E]), tri8_sb[:, :, :], ALU.mult))
            step(6, nc.vector.reduce_sum(tile_end[:, :], upto[:, :, :], AX.X))
            step(7, nc.vector.tensor_tensor(past[:, :, :], tid_sb[:, :].unsqueeze(2).to_broadcast([1, TABLE, E]),
                                            tile_end[:, :].unsqueeze(1).to_broadcast([1, TABLE, E]), ALU.is_ge))
            nc.vector.reduce_sum(t_exp[:, :], past[:, :, :], AX.X).then_inc(s_tab, 1)
            step(9, nc.vector.tensor_tensor(past_n[:, :, :], past[:, :, :], n_tiles[:, :].unsqueeze(1).to_broadcast([1, TABLE, E]), ALU.mult))
            nc.vector.tensor_scalar(tab_e[:, 1:1 + TABLE], t_exp[:, :], float(E - 1), None, ALU.min).then_inc(s_tab, 1)
            step(11, nc.vector.reduce_sum(t_first[:, :], past_n[:, :, :], AX.X))
            step(12, nc.vector.scalar_tensor_tensor(out=t_row[:, :], in0=t_first[:, :], scalar=-float(TR), in1=tslot_sb[:, :],
                                                    op0=ALU.mult, op1=ALU.add))
            step(13, nc.vector.scalar_tensor_tensor(out=tab_row[:, :], in0=t_exp[:, :], scalar=float(REGION), in1=t_row[:, :],
                                                    op0=ALU.mult, op1=ALU.add))
            dve.wait_ge(s_mix, 1)
            nc.vector.tensor_tensor(x_sb[:, :, :], x_sb[:, :, :], b2_sb[:, E:E + 1, :].to_broadcast([P, B * NT, C]), ALU.add).then_inc(s_b2s, 1)
            dve.wait_ge(s_b2s, 1)
            for b in range(1, EARLY):
                add_shared(b)

            HALF = RING // 2
            expert_regs = [[dve.alloc_register(f"expert{half}_{n}") for n in range(HALF + AHEAD)] for half in range(2)]

            def load_half(it, half):
                dve.load(expert_regs[half], tab_e[0:1, bass.ds(it * RING + HALF * half, HALF + AHEAD)])

            def expert(u, tile):
                return dve.snap(expert_regs[u // HALF][u % HALF + tile + 1], min_val=0, max_val=E - 1)

            def copy_w1(v, e):
                nc.vector.tensor_copy(w1_cur[:, v, :], w1_sb[:, e, :])
                nc.vector.tensor_copy(b1_cur[:, v, :], b1_sb[:, e, :]).then_inc(s_w1c, 1)

            def copy_w2(v, e):
                nc.vector.tensor_copy(w2_cur[v], w2_sb[:, e, :, :]).then_inc(s_w2c, 1)

            def tile_yT(t, par):
                dve.wait_ge(s_tT, t + 1)
                wait(dve, s_tup, (t - 1) * (FC // 2))
                nc.vector.tensor_copy(yT_tile[:, par, :], ps[:, BK_TT + par, 0:TR]).then_inc(s_tyT, 1)

            def tile_result(t, v, before, u, e):
                wait(dve, s_res[v], before * (16 * TH))
                nc.vector.tensor_copy(row_id[:, v, :], y_tile[:, u, :, C].bitcast(u32)).then_inc(s_rid, 1)
                dve.wait_ge(s_tdn, t + 1)
                nc.vector.tensor_tensor(r_tile[:, v, :, :], ps[:, BK_TD + v % 2, 0:TH * C].rearrange("p (h c) -> p h c", c=C),
                                        b2_sb[:, bass.ds(e, 1), :].to_broadcast([P, TH, C]), ALU.add).then_inc(s_rt2, 1)

            def tile_step(it, u):
                t = it * RING + u
                left = TILES - t if isinstance(t, int) else TILES
                if not (isinstance(t, int) and t == 0):
                    before = (t - 1) // TQ if isinstance(t, int) else it * (RING // TQ) + (u - 1) // TQ
                    tile_result(t - 1, (u - 1) % TQ, before, (u - 1) % RING, expert(u, -1))
                if left > 2:
                    tile_yT(t + 2, u % 2)
                if left > 3:
                    copy_w2((u + 3) % TQ, expert(u, 3))
                if left > 4:
                    dve.wait_ge(s_th, (t + 1) * FC)
                    copy_w1(u % TQ, expert(u, 4))
                if u == 1:
                    load_half(it, 1)
                elif u == HALF + 1 and left > RING:
                    load_half(it + 1, 0)

            load_half(0, 0)
            for v in range(TQ):
                copy_w1(v, expert(0, v))
                if v < 3:
                    copy_w2(v, expert(0, v))
                if v < 2:
                    tile_yT(v, v)
            for u in range(RING):
                tile_step(0, u)
            with dve.Fori(1, TABLE // RING - 1) as it:
                for u in range(RING):
                    tile_step(it, u)
            for t in range(TABLE - RING, TILES):
                tile_step(TABLE // RING - 1, t % RING)
            t = TILES - 1
            tile_result(t, t % TQ, t // TQ, t % RING, expert(t % RING, 0))

            dve.wait_ge(s_ge, 1)
            nc.vector.tensor_scalar(l_sum[:, :], l_exp[:, :], 1.0, None, ALU.add).then_inc(s_gate, 1)
            dve.wait_ge(s_gate, 1)
            nc.vector.reciprocal(top_p[:, 0, :], l_sum[:, :]).then_inc(s_gate, 1)
            dve.wait_ge(s_gate, 2)
            nc.vector.tensor_tensor(top_p[:, 1, :], l_exp[:, :], top_p[:, 0, :], ALU.mult).then_inc(s_gate, 1)
            dve.wait_ge(s_gate, 3)

            def combine(b, n):
                if b < EARLY or ORDER.index(("shared", b)) < ORDER.index(("routed", b)):
                    dve.wait_ge(s_mix, b + 1)
                dve.wait_ge(s_rl[b], 16)
                for k in range(K2):
                    if k:
                        dve.wait_ge(s_part, n + 1)
                    for t in range(NT * b, NT * (b + 1)):
                        last = nc.vector.scalar_tensor_tensor(
                            out=x_sb[:, t, :], in0=r_seq[b][:, t % NT, k, :], scalar=top_p[:, k, t:t + 1],
                            in1=x_sb[:, t, :], op0=ALU.mult, op1=ALU.add)
                    last.then_inc(s_fin if k else s_part, 1)

            for kind, b in ORDER:
                if kind == "routed":
                    combine(b, BY_DVE.index(b))
                else:
                    if ("routed", b) in ORDER[:ORDER.index((kind, b))]:
                        dve.wait_ge(s_fin, BY_DVE.index(b) + 1)
                    add_shared(b)

        @block.tensor
        def _(pe):
            pe.wait_ge(s_w1st, 16 * N_W1ST)

            def transpose_x(b, par):
                pe.wait_ge(s_xn, b + 1)
                wait(pe, s_xnT, b - 1)
                for i in range(NT):
                    last = nc.tensor.transpose(ps[:, par, P * i:P * (i + 1)], xn[:, par, i, :], id_sb[:, :])
                last.then_inc(s_xnTp, 1)

            def project(b, par):
                pe.wait_ge(s_xnT, b + 1)
                wait(pe, s_qk32, 2 * (b - 1))
                nc.tensor.matmul(ps[:, 2 + par, :], wq_sb[:, :], xnT[:, par, :], start=True, stop=True).then_inc(s_qp, 1)
                nc.tensor.matmul(ps[:, 4 + par, :], wk_sb[:, :], xnT[:, par, :], start=True, stop=True).then_inc(s_kp, 1)
                if not (isinstance(b, int) and b == B - 1):
                    transpose_x(b + 1, 1 - par)
                wait(pe, s_v, b - 1)
                for i in range(NT):
                    last = nc.tensor.matmul(ps[:, 6 + par, C * i:C * (i + 1)], xnT[:, par, P * i:P * (i + 1)], wv_sb[:, :],
                                            start=True, stop=True)
                last.then_inc(s_vp, 1)

            transpose_x(0, 0)
            project(0, 0)
            project(1, 1)
            with pe.Fori(1, B // 2 - 1) as it:
                project(it * 2, 0)
                project(it * 2 + 1, 1)
            project(B - 2, 0)
            project(B - 1, 1)

            pe.wait_ge(s_qk32, 2 * B)

            def row_scores(b, hg, a):
                j, i = a // NT, a % NT
                if a == 0:
                    pe.wait_ge(s_ld[hg], (b + 1) * (16 * N_LD))
                if a % 2 == 0:
                    wait(pe, s_max, (b * HG + hg) * (J * NT // 2) + a // 2 - 1)
                last = nc.tensor.matmul(ps[:, BK_A + a % 4, :], q_op[hg][0:SH, j, P * i:P * (i + 1)], k_op[hg][0:SH, j, :],
                                        start=True, stop=True)
                if a % 2:
                    last.then_inc(s_sa, 1)

            def key_scores(b, hg, i, j):
                n = (b * HG + hg) * (J * NT) + i * J + j
                if i == 0 and j == 0:
                    pe.wait_ge(s_sh[hg], (b + 1) * (16 * SHIFTS))
                if key_banks(b, hg) == 2:
                    wait(pe, s_exp, n - 1)
                elif i > 0 or hg == HG - 1:
                    pe.wait_ge(s_exp, n - J + 1)
                elif j < 2:
                    pe.wait_ge(s_exp, n - 1)
                else:
                    pe.wait_ge(s_max, NG * (J * NT // 2))
                nc.tensor.matmul(ps[:, BK_S + j % key_banks(b, hg), :], k_op[hg][:, j, P * i:P * (i + 1)], q_op[hg][:, j, :],
                                 start=True, stop=True).then_inc(s_sb, 1)

            def pv(b, hg, i):
                g = b * HG + hg
                pe.wait_ge(s_exp, g * (J * NT) + (i + 1) * J)
                if i == 0:
                    wait(pe, s_ot, g)
                    pe.wait_ge(s_vop, g + 1)
                for j in range(J):
                    last = nc.tensor.matmul(ps[32 * j:32 * j + 32, BK_O, :], v_op[:, hg, i, j, :], probs[:, i, j, :],
                                            start=(i == 0), stop=(i == NT - 1))
                last.then_inc(s_pv, 1)

            def max_rows(b, hg):
                g = b * HG + hg
                pe.wait_ge(s_msp, g + 1)
                wait(pe, s_mxT, g)
                if hg == 2:
                    wait(pe, s_x2, b)
                if hg == 0 and not (isinstance(b, int) and b < 2):
                    pe.wait_ge(s_rt, (b - 2) * R + 1)
                if hg == 1 and not (isinstance(b, int) and b < 1):
                    pe.wait_ge(s_cn, b * Q)
                nc.tensor.transpose(ps[:, BK_M, 0:P // 2].bitcast(bf16), mx_parts[:, :], id_bf[:, :]).then_inc(s_mxTp, 1)

            def project_out(b, i):
                if i == 0:
                    pe.wait_ge(s_wo, 16 * J)
                    pe.wait_ge(s_o, b + 1)
                    last_b = isinstance(b, int) and b == B - 1
                    pe.wait_ge(s_mxT, NG if last_b else (b + 1) * HG + 2)
                    if last_b:
                        pe.wait_ge(s_cn, (b + 1) * Q)
                last = nc.tensor.matmul(ps[:, BK_M, C * i:C * (i + 1)], o_sb[:, P * i:P * (i + 1)], wo_sb[:, :],
                                        start=True, stop=True)
                if i == NT - 1:
                    last.then_inc(s_ap, 1)

            def transpose_y(b):
                pe.wait_ge(s_yn, b + 1)
                last_b = isinstance(b, int) and b == B - 1
                if last_b:
                    pe.wait_ge(s_x2, B)
                else:
                    pe.wait_ge(s_mxT, (b + 2) * HG)
                for i in range(NT):
                    last = nc.tensor.transpose(ps[:, BK_M, P * i:P * (i + 1)], y2[:, i, 0, 0:C], id_sb[:, :])
                last.then_inc(s_yTp, 1)

            def router(b):
                pe.wait_ge(s_yT, b + 1)
                for i in range(NT):
                    last = nc.tensor.matmul(ps[:, BK_M, E * i:E * (i + 1)], yT_now[:, P * i:P * (i + 1)], wr_sb[:, :],
                                            start=True, stop=True)
                last.then_inc(s_lgp, 1)

            def ranks(b):
                pe.wait_ge(s_rt, (b + 1) * R)
                pe.wait_ge(s_cn, (b + 1) * Q)
                last_mx = NG if isinstance(b, int) and b >= B - 2 else (b + 2) * HG + 1
                pe.wait_ge(s_mxT, last_mx)
                n = NC * E
                nc.tensor.matmul(ps[:, BK_M, 0:n], tri_bf[:, :], chosen[:, :, :].rearrange("p c e -> p (c e)"),
                                 start=True, stop=False)
                for d in range(1, NC):
                    nc.tensor.matmul(ps[:, BK_M, E * d:n], ones_bf[:, :],
                                     chosen[:, 0:NC - d, :].rearrange("p c e -> p (c e)"), start=False, stop=False)
                every = ps[:, BK_M, 0:n].rearrange("p (c e) -> p c e", e=E)
                nc.tensor.matmul(every, ones_bf[:, :], run_bf[:, :].unsqueeze(1).to_broadcast([P, NC, E]), start=False, stop=False)
                nc.tensor.matmul(every, ones_bf[:, :], reg_bf[:, :].unsqueeze(1).to_broadcast([P, NC, E]),
                                 start=False, stop=True).then_inc(s_rk, 1)

            for hg in range(2):
                for a in range(J * NT):
                    row_scores(0, hg, a)
                    if hg == 1 and a == 7:
                        pe.wait_ge(s_xnT, B)
                        pe.wait_ge(s_v, B)
                        pe.wait_ge(s_w, 16 * N_W)
                        pe.wait_ge(s_idbf, 2)
                        max_rows(0, 0)
            pe.wait_ge(s_tab, N_MAT)

            def attend(b):
                first, last_b = isinstance(b, int) and b == 0, isinstance(b, int) and b == B - 1
                for hg in range(HG):
                    for s in range(J * NT):
                        key_scores(b, hg, s // J, s % J)
                        for a in ROW_TILES[s % J]:
                            if hg < HG - 2:
                                row_scores(b, hg + 2, s // J * J + a)
                            elif not last_b:
                                row_scores(b + 1, hg - 2, s // J * J + a)
                        if s == MX_STEP:
                            if hg < HG - 1:
                                max_rows(b, hg + 1)
                            elif not last_b:
                                max_rows(b + 1, 0)
                        if s % J == PV_LAG % J:
                            i = (s - PV_LAG) // J
                            if i >= 0:
                                pv(b, hg, i)
                            elif hg > 0:
                                pv(b, hg - 1, NT + i)
                            elif not first:
                                pv(b - 1, HG - 1, NT + i)
                        if not first:
                            if hg == 1 and s in (0, 1, 2, 3):
                                project_out(b - 1, s)
                            if hg == 2 and s == YT_STEP:
                                transpose_y(b - 1)
                            if hg == 3 and s == 1:
                                router(b - 1)
                            if hg == 3 and s == 14:
                                ranks(b - 1)

            sequences(pe, attend)
            for i in range((J * NT - PV_LAG + J - 1) // J, NT):
                pv(B - 1, HG - 1, i)
            for i in range(NT):
                project_out(B - 1, i)

            pe.wait_ge(s_wffn, 16 * N_WFFN)
            pe.wait_ge(s_exp, NG * J * NT)
            pe.wait_ge(s_max, NG * J * NT // 2)

            def up(b):
                for c in range(FC):
                    wait(pe, s_gelu, (b - 1) * FC + c + 1)
                    if c == 0:
                        pe.wait_ge(s_kept, b + 1)
                    nc.tensor.matmul(ps[:, UP0 + c, :], w1_sb[:, E, P * c:P * (c + 1)], yT[:, b, :],
                                     start=True, stop=True).then_inc(s_up, 1)

            def down(b):
                pe.wait_ge(s_gelu, (b + 1) * FC)
                wait(pe, s_mix, b - 1)
                for i in range(NT):
                    for c in range(FC):
                        last = nc.tensor.matmul(ps[:, DN0 + b % 2, C * i:C * (i + 1)], hid[:, b % 2, c, P * i:P * (i + 1)],
                                                w2_sb[:, E, c, :], start=(c == 0), stop=(c == FC - 1))
                last.then_inc(s_dn, 1)

            up(0)
            up(1)
            transpose_y(B - 1)
            down(0)
            router(B - 1)
            up(2)
            ranks(B - 1)
            pe.wait_ge(s_cn, (B + 1) * Q)
            nc.tensor.matmul(ps[:, BK_M, 0:E], ones_bf[:, :], run_bf[:, :], start=True, stop=True).then_inc(s_cntp, 1)
            down(1)
            for b in range(2, EARLY):
                if b + 1 < EARLY:
                    up(b + 1)
                down(b)

            pe.wait_ge(s_gelu, EARLY * FC)
            pe.wait_ge(s_mix, EARLY)
            pe.wait_ge(s_tab, N_MAT + 1)

            def tile_T(it, u):
                t = it * RING + u
                par = u % 2
                pe.wait_ge(s_yl[u % RING], (it + u // RING + 1) * 16)
                wait(pe, s_tyT, t - 1)
                for h in range(TH):
                    last = nc.tensor.transpose(ps[:, BK_TT + par, P * h:P * (h + 1)], y_tile[:, u % RING, h, 0:C], id_sb[:, :])
                last.then_inc(s_tT, 1)

            def tile_up(t, v):
                par = v % 2
                pe.wait_ge(s_tyT, t + 1)
                pe.wait_ge(s_w1c, t + 1)
                for c in range(FC):
                    if c % 2 == 0:
                        wait(pe, s_th, (t - 2) * FC + c + 2)
                    last = nc.tensor.matmul(ps[:, BK_TU + 2 * par + c // 2, TR * (c % 2):TR * (c % 2 + 1)],
                                            w1_cur[:, v, P * c:P * (c + 1)], yT_tile[:, par, :], start=True, stop=True)
                    if c % 2:
                        last.then_inc(s_tup, 1)

            def tile_down(t, v):
                par = v % 2
                pe.wait_ge(s_w2c, t + 1)
                pe.wait_ge(s_th, (t + 1) * FC)
                wait(pe, s_rt2, t - 1)
                for h in range(TH):
                    for c in range(FC):
                        last = nc.tensor.matmul(ps[:, BK_TD + par, C * h:C * (h + 1)], hid_tile[:, par, c, P * h:P * (h + 1)],
                                                w2_cur[v][:, c, :], start=(c == 0), stop=(c == FC - 1))
                last.then_inc(s_tdn, 1)

            def tile_step(it, u):
                t = it * RING + u
                left = TILES - t if isinstance(t, int) else TILES
                if left > 1:
                    tile_up(t + 1, (u + 1) % TQ)
                if left > 2:
                    tile_T(it, u + 2)
                tile_down(t, u % TQ)

            tile_T(0, 0)
            tile_T(0, 1)
            tile_up(0, 0)
            for u in range(RING):
                tile_step(0, u)
            with pe.Fori(1, TABLE // RING - 1) as it:
                for u in range(RING):
                    tile_step(it, u)
            for t in range(TABLE - RING, TILES):
                tile_step(TABLE // RING - 1, t % RING)

            pe.wait_ge(s_th, TILES * FC)
            pe.wait_ge(s_tyT, TILES)
            up(EARLY)
            for b in range(EARLY, B):
                if b + 1 < B:
                    up(b + 1)
                down(b)


def kernel(**a):
    import numpy as np
    import concourse.bacc as bacc
    from concourse import mybir as mb
    from concourse.bass_utils import run_bass_kernel_spmd as run

    a = {k.replace("L0_attn_", "a_").replace("L0_ffn_", "f_"): np.asarray(v) for k, v in a.items()}
    with_shared = lambda routed, shared: np.concatenate([routed, shared[None]], axis=0)
    ins = {
        "x": a["a_x"].reshape(B * S, C),
        "WqT": a["a_Wq"].T, "WkT": a["a_Wk"].T, "WvT": a["a_Wv"].T, "WoT": a["a_Wo"].T,
        "bq": a["a_bq"], "bk": a["a_bk"], "bv": a["a_bv"], "bo": a["a_bo"], "head_mask": a["a_head_mask"],
        "W1": with_shared(a["f_Wfc"], a["f_Wfc_s"]).transpose(1, 0, 2),
        "b1": with_shared(a["f_bfc"], a["f_bfc_s"]).reshape(NE, FC, P).transpose(2, 0, 1),
        "W2": with_shared(a["f_Wproj"], a["f_Wproj_s"]).reshape(NE, FC, P, C).transpose(2, 0, 1, 3),
        "b2": with_shared(a["f_bproj"], a["f_bproj_s"]),
        "Wr": a["f_Wr"],
        "ident": np.eye(P, dtype=np.float32),
        "tri": np.triu(np.ones((P, P), np.float32), 1),
        "region_at": np.concatenate([np.arange(E, dtype=np.float32)[None] * REGION, np.zeros((P - 1, E), np.float32)]),
        "region_row": np.arange(E, dtype=np.float32)[None] * REGION,
        "row_ids": np.arange(K2 * B * S, dtype=np.uint32).reshape(B * S, K2),
        "dump_ids": (K2 * B * S + np.arange(K2 * E * TR, dtype=np.uint32)).reshape(K2 * E, TH, P, 1).transpose(2, 0, 1, 3),
        "thresholds": np.arange(0, B * S, TR, dtype=np.float32)[None],
        "tri8": np.tril(np.ones((E, E), np.float32))[None],
        "tile_slots": np.arange(TABLE, dtype=np.float32)[None] * TR,
        "tile_ids": np.arange(TABLE, dtype=np.float32)[None],
        "iota8": np.tile(np.arange(E, dtype=np.float32), (P, 1)),
    }
    nc = bacc.Bacc("TRN2", target_bir_lowering=False, num_devices=1)
    arrays, aps = {}, {}
    for name, v in ins.items():
        v = np.ascontiguousarray(v)
        arrays[f"in_{name}"] = v
        aps[name] = nc.dram_tensor(f"in_{name}", v.shape, mb.dt.from_np(v.dtype), kind="ExternalInput").ap()
    aps["out"] = nc.dram_tensor("out_0", (B * S, C), mb.dt.float32, kind="ExternalOutput").ap()
    block_kernel(nc, **aps)
    r = run(nc, [arrays], core_ids=[0])
    return r.results[0]["out_0"].reshape(B, S, C)
```
